# Optimizing a Trainium2 kernel written in Bass

```python
import numpy as np
import jax
import jax.numpy as jnp

def _softmax(x, axis=-1):
    return jax.nn.softmax(x, axis=axis)

def _gelu(x):
    return jax.nn.gelu(x, approximate=True)

def _silu(x):
    return jax.nn.silu(x)

def _sigmoid(x):
    return jax.nn.sigmoid(x)

def _layernorm(x, axis=-1, eps=1e-05):
    m = jnp.mean(x, axis=axis, keepdims=True)
    v = jnp.var(x, axis=axis, keepdims=True)
    return (x - m) / jnp.sqrt(v + eps)

def _scatter_add(tgt, idx, src, axis=0):
    return tgt.at[idx].add(src)

def _segment_sum(src, seg, n):
    return jax.ops.segment_sum(src, seg, n)
kernel_name = 'mk_adj_preln_d1_adj_r2_b8da49'

def setup_inputs(seed: int=0):
    np.random.seed(seed)
    _w = jnp.asarray

    def _rec_inputs():
        import jax
        import jax.numpy as jnp
        _gk = jax.random.key(seed)
        x = 7.22e-05 + 1 * jax.random.normal(jax.random.fold_in(_gk, 1), (32, 256, 1024), jnp.float32)
        _w = (1.0 + jnp.arange(256, dtype=jnp.float32)) ** (-0.5)
        _w = _w / _w.mean()
        _pij = jnp.clip(0.0078125 * _w[:, None] * _w[None, :], 0.0, 1.0)
        _a = jax.random.uniform(jax.random.fold_in(_gk, 2), (256, 256)) < _pij
        _a = jnp.logical_or(_a, jnp.swapaxes(_a, -1, -2))
        _a = jnp.logical_or(_a, jnp.eye(256, dtype=bool))
        _af = _a.astype(jnp.float32)
        _af = _af * jax.random.uniform(jax.random.fold_in(_gk, 3), (256, 256), jnp.float32, 0.05, 0.0885215)
        adj = _af
        return (x, adj)
    x, adj = _rec_inputs()

    def _L0_gnn_setup():
        import jax, jax.numpy as jnp
        import numpy as np
        B, S, N = (8, 256, 1024)
        HID = 256
        K = 8

        def _construct_adj(x, k):
            Bn, Sn, Nn = x.shape
            fv = x.mean(axis=1)
            nf = fv / jnp.linalg.norm(fv, axis=1, keepdims=True)
            sim = nf[:, :, None] * nf[:, None, :]
            kk = min(k, Nn - 1)
            _, idx = jax.lax.top_k(sim, kk + 1)
            idx = idx[..., 1:]
            b_ix = jnp.arange(Bn)[:, None, None]
            r_ix = jnp.arange(Nn)[None, :, None]
            adj = jnp.zeros((Bn, Nn, Nn), x.dtype).at[b_ix, r_ix, idx].set(1.0)
            adj = jnp.maximum(adj, jnp.swapaxes(adj, 1, 2))
            d = jnp.arange(Nn)
            adj = adj.at[:, d, d].set(1.0)
            return adj

        def _gc(x, adj, W, b):
            deg = adj.sum(axis=2, keepdims=True)
            deg = jnp.where(deg == 0, jnp.ones_like(deg), deg)
            h = x @ W.T + b
            return jnp.einsum('bij,bjh->bih', adj / deg, h)
        key = jax.random.key(seed)
        k0, k1, k2 = jax.random.split(key, 3)
        x = jax.random.normal(k0, (B, S, N), jnp.float32)
        W1 = jax.random.normal(k1, (HID, S), jnp.float32) * 0.02
        b1 = jnp.zeros((HID,), jnp.float32)
        W2 = jax.random.normal(k2, (S, HID), jnp.float32) * 0.02
        b2 = jnp.zeros((S,), jnp.float32)
        return {'x': x, 'W1': W1, 'b1': b1, 'W2': W2, 'b2': b2}
    _L0_gnn_all = _L0_gnn_setup()
    _L0_gnn_in = {k: v for k, v in _L0_gnn_all.items() if k in ('b1', 'b2')}
    del _L0_gnn_all
    return {'x': x, 'adj': adj, 'L0_gnn_b1': _L0_gnn_in['b1'], 'L0_gnn_b2': _L0_gnn_in['b2']}

def reference(x, adj, L0_gnn_b1, L0_gnn_b2):
    import jax
    import jax.numpy as jnp

    def _L0_gnn_ref(x, W1, b1, W2, b2):
        import jax, jax.numpy as jnp
        import numpy as np
        B, S, N = (8, 256, 1024)
        HID = 256
        K = 8

        def _construct_adj(x, k):
            Bn, Sn, Nn = x.shape
            fv = x.mean(axis=1)
            nf = fv / jnp.linalg.norm(fv, axis=1, keepdims=True)
            sim = nf[:, :, None] * nf[:, None, :]
            kk = min(k, Nn - 1)
            _, idx = jax.lax.top_k(sim, kk + 1)
            idx = idx[..., 1:]
            b_ix = jnp.arange(Bn)[:, None, None]
            r_ix = jnp.arange(Nn)[None, :, None]
            adj = jnp.zeros((Bn, Nn, Nn), x.dtype).at[b_ix, r_ix, idx].set(1.0)
            adj = jnp.maximum(adj, jnp.swapaxes(adj, 1, 2))
            d = jnp.arange(Nn)
            adj = adj.at[:, d, d].set(1.0)
            return adj

        def _gc(x, adj, W, b):
            deg = adj.sum(axis=2, keepdims=True)
            deg = jnp.where(deg == 0, jnp.ones_like(deg), deg)
            h = x @ W.T + b
            return jnp.einsum('bij,bjh->bih', adj / deg, h)
        adj = _construct_adj(x, K)
        xr = jnp.swapaxes(x, 1, 2)
        h = jax.nn.relu(_gc(xr, adj, W1, b1))
        h = _gc(h, adj, W2, b2)
        return jnp.swapaxes(h, 1, 2)
    h = jnp.maximum(_layernorm(x, axis=-1), 0.0)
    x = x + _L0_gnn_ref(h, adj, L0_gnn_b1, adj, L0_gnn_b2)
    return x

_drawn_inputs = setup_inputs


def setup_inputs(seed=0):
    import zlib

    import numpy as np

    out = dict(_drawn_inputs(seed))
    spreads = {'L0_gnn_b1': (0.0, 0.555), 'L0_gnn_b2': (0.0, 0.1)}
    factors = {}
    for name, (base, spread) in spreads.items():
        noise = np.random.default_rng([zlib.crc32(name.encode()), seed]).standard_normal(out[name].shape)
        drawn = base * np.exp(spread * noise) if base else spread * noise
        out[name] = jnp.asarray(drawn.astype(out[name].dtype))
    for name, factor in factors.items():
        out[name] = (out[name] * factor).astype(out[name].dtype)
    return out
```

```python
import concourse.bass as bass
from concourse import mybir
from concourse.alu_op_type import AluOpType as ALU
from contextlib import ExitStack

ACT = mybir.ActivationFunctionType
AX = mybir.AxisListType
F32 = mybir.dt.float32
F32R = mybir.dt.float32r
BF16 = mybir.dt.bfloat16

B, S, N = 32, 256, 1024
P = 128
KC = S // P
HALF = 512
NH = N // HALF
GB = 2
NG = B // GB
RING = 3
CH = GB * KC
UNITS = GB * NH
TOPK = 8
NC = 8
ROWS = 32
R = GB * ROWS
PARTS = 2
NU = TOPK
U0 = 1
DEG = float(TOPK + 1)
EPS = 1e-5
BIG = 2.0 ** 100
PAD = 8


def node_class_constants():
    import numpy as np

    lanes = np.arange(R)
    cls, part = lanes % NC, (lanes % ROWS) // NC
    want = np.zeros((P, 2), np.float32)
    want[:R, 0] = cls
    want[:R, 1] = np.where(part == 1, -1, 0)
    const = np.array([DEG, N, DEG, N + 1, DEG, N, 0, N], np.float32)
    coef = np.zeros((NC, NC), np.float32)
    coef[[2, 6], 1] = -1
    coef[[2, 3], 3] = -1
    coef[[2, 6], 4] = 1
    coef[[2, 3, 6, 7, 4, 5], 6] = 1
    pick = np.zeros((P, 2, GB, NC), np.float32)
    for p in range(R):
        if part[p] == 0:
            b = p // ROWS
            pick[p, 0, b, cls[p]] = 1
            pick[p, 1, b, :] = coef[cls[p]]
    base = np.zeros((P, 2, GB, NC), np.float32)
    base[:, 1] = const
    cut = np.zeros((P, P), np.float32)
    cut[:R][(part == 0) & (cls % 4 != 0)] = -BIG
    return np.concatenate([want, pick.reshape(P, -1), base.reshape(P, -1), cut], 1)


MID = 10
LATE = 5
TK = 9

C_WANT, C_NEG, C_PICK = 0, 1, 2
C_BASE = C_PICK + 2 * GB * NC
C_CUT = C_BASE + 2 * GB * NC
C_ALL = C_CUT + P


def gnn_kernel(nc, x, adj_t, bias1, bias2, consts, out):
    x_v = x.rearrange("b (k p) n -> b p k n", p=P)
    out_v = out.rearrange("b (k p) n -> b p k n", p=P)
    t_rows = nc.dram_tensor("t_rows", (B, N), BF16, kind="Internal").ap()

    with ExitStack() as ctx:
        def sb(name, shape, dt=F32):
            return ctx.enter_context(nc.sbuf_tensor(name, shape, dt))

        def sem(name):
            return ctx.enter_context(nc.semaphore(name))

        xs = sb("xs", [P, RING, GB, KC, N])
        hi = sb("hi", [P, RING, GB, KC, N], F32R)
        lo = sb("lo", [P, RING, GB, KC, N], F32R)
        hf = sb("hf", [P, KC, N])
        y1 = sb("y1", [P, 2, KC, HALF])
        ob = sb("ob", [P, GB, KC, N])
        wt = sb("wt", [P, KC, S])
        wh = sb("wh", [P, KC, S], F32R)
        wl = sb("wl", [P, KC, S], F32R)
        cs = sb("cs", [P, C_ALL])
        b1 = sb("b1", [P, KC])
        b2 = sb("b2", [R, S])
        cut = sb("cut", [R, P], F32R)
        sums = sb("sums", [P, GB, R], F32R)
        spare = sb("spare", [P, 8])
        ones = sb("ones", [R, P])
        fv = sb("fv", [R, N + PAD])
        top = sb("top", [R, 2, 8])
        code = sb("code", [R, N], BF16)
        tr = sb("tr", [R, N], BF16)
        onehot = sb("onehot", [R, RING, N], F32R)
        count = sb("count", [R, RING])
        count_r = sb("count_r", [R, RING, 2 * GB * NC])
        tmap = sb("tmap", [P, GB, N], BF16)
        junk = sb("junk", [P, 2, N], BF16)
        bn = sb("bn", [P, KC, 2, 6])
        mv = sb("mv", [P, RING, GB, KC, 2])
        var = sb("var", [P, GB, KC])
        std = sb("std", [P, GB, KC])
        nw = sb("nw", [P, 4, KC])
        rstd = sb("rstd", [P, RING, GB, KC])
        nbias = sb("nbias", [P, GB, KC])
        s_all = sb("s_all", [P, RING, GB, KC])
        s_max = sb("s_max", [P, GB, KC])
        s_t = sb("s_t", [P, GB, KC])
        s_u = sb("s_u", [P, 3, GB, KC])
        nd = sb("nd", [P, RING, 2, GB, NC])
        rdeg = sb("rdeg", [P, RING, GB, NC])
        rdeg9 = sb("rdeg9", [P, RING, GB, NC])
        q1 = sb("q1", [P, KC, GB, NC])
        bv = sb("bv", [P, RING, KC, GB, NC])
        v1 = sb("v1", [P, RING, KC, GB, NC])
        nv = sb("nv", [P, KC, GB, NC])
        pt = sb("pt", [P, 6, KC, GB])
        p2 = sb("p2", [P, RING, KC, GB, NC])
        acc = sb("acc", [P, RING, KC, GB, NH])
        yu = sb("yu", [P, RING, KC, GB, NU])
        yus = sb("yus", [P, RING, KC, GB])
        wrong = sb("wrong", [P, KC, GB])
        snk = sb("snk", [P, 3, KC, GB])
        q2 = sb("q2", [P, KC, GB, ROWS])
        rx = sb("rx", [R, S])
        rh = sb("rh", [R, S], F32R)
        l2w = sb("l2w", [R, S], F32R)

        ps = [ctx.enter_context(nc.psum_tensor(f"ps{i}", [P, KC, HALF], F32)) for i in range(3)]
        pf = ctx.enter_context(nc.psum_tensor("pf", [P, N], F32))
        pf_n = pf[:, 0:2 * GB * NC]
        pf_q = pf[:, 64:64 + KC * GB * NC].rearrange("p (m c) -> p m c", m=KC)
        pf_w = pf[0:R, HALF:HALF + S]

        x_in = [[sem(f"x_in{s}{b}") for b in range(GB)] for s in range(RING)]
        loaded = sem("loaded")
        const_ready = sem("const_ready")
        b2_ready = sem("b2_ready")
        w_hi = sem("w_hi")
        w_ready = sem("w_ready")
        stats_done = sem("stats_done")
        mv_done = sem("mv_done")
        mv_ready = sem("mv_ready")
        std_ready = sem("std_ready")
        newton = sem("newton")
        coef_ready = sem("coef_ready")
        h_ready = sem("h_ready")
        hi_ready = sem("hi_ready")
        lo_ready = sem("lo_ready")
        fv_ready = sem("fv_ready")
        fv_copied = sem("fv_copied")
        topk = sem("topk")
        t_ready = sem("t_ready")
        class_ready = sem("class_ready")
        count_ready = sem("count_ready")
        t_saved = sem("t_saved")
        t_spread = sem("t_spread")
        st_done = sem("st_done")
        n_ready = sem("n_ready")
        mid = sem("mid")
        q1_ready = sem("q1_ready")
        wq1_ready = sem("wq1_ready")
        bv_ready = sem("bv_ready")
        pool_step = sem("pool_step")
        p2_ready = sem("p2_ready")
        l1_ps = sem("l1_ps")
        l1_out = sem("l1_out")
        yu_fixed = sem("yu_fixed")
        hi2_ready = sem("hi2_ready")
        lo2_ready = sem("lo2_ready")
        late = sem("late")
        q2_ready = sem("q2_ready")
        wq2_ready = sem("wq2_ready")
        l2w_step = sem("l2w_step")
        l2w_ready = sem("l2w_ready")
        l2_ps = sem("l2_ps")
        done = sem("done")
        stored = [sem(f"stored{b}") for b in range(GB)]

        def some(value):
            return not isinstance(value, int) or value > 0

        def hold(dve, s, value, column):
            dve.wait_ge(s, value)
            dve.memset(spare[:, column:column + 1], 0.0)

        def after(g, slot, lap, d):
            return g + d, (slot + d) % RING, lap + (slot + d) // RING

        def schedule(eng, body):
            body(-2, 1, -1, False, False, True)
            body(-1, 2, -1, False, True, True)
            body(0, 0, 0, True, True, True)
            laps = (NG - 3) // RING
            with eng.Fori(0, laps) as i:
                for j in range(RING):
                    g, slot = 3 * i + (1 + j), (1 + j) % RING
                    body(g, slot, i + (1 + j) // RING, True, True, True)
            for g in range(1 + RING * laps, NG):
                body(g, g % RING, g // RING, True, g + 1 < NG, g + 2 < NG)

        block = ctx.enter_context(nc.Block())

        @block.sync
        def _(sp):
            for dst, src in ((wt[:], adj_t.rearrange("(k p) o -> p k o", p=P)), (cs[:], consts),
                             (b1[:], bias1), (b2[:], bias2.to_broadcast([R, S]))):
                sp.dma_start(dst, src).then_inc(loaded, 16)

            def load(g, slot, b):
                sp.dma_start(xs[:, slot, b], x_v[g * GB + b]).then_inc(x_in[slot][b], 16)

            for g in range(RING):
                for b in range(GB):
                    load(g, g, b)

            def body(g, slot, lap, main, mid_, prep):
                def store(b):
                    sp.wait_ge(done, UNITS * g + NH * (b + 1))
                    sp.dma_start(out_v[g * GB + b], ob[:, b]).then_inc(stored[b], 16)

                if main:
                    store(0)
                    if not isinstance(g, int) or g + RING < NG:
                        load(g + RING, slot, 0)
                if prep:
                    p = g + 2
                    sp.wait_ge(t_ready, p + 1)
                    sp.dma_start(t_rows[bass.ds(p * GB, GB)], tr[0:R:ROWS, :]).then_inc(t_saved, 16)
                if main:
                    store(1)
                    if not isinstance(g, int) or g + RING < NG:
                        load(g + RING, slot, 1)
                if prep:
                    sp.wait_ge(t_saved, 16 * (p + 1))
                    if some(GB * p):
                        sp.wait_ge(st_done, GB * p)
                    for b in range(GB):
                        sp.dma_start(tmap[:, b], t_rows[bass.ds(p * GB + b, 1)].to_broadcast([P, N])
                                     ).then_inc(t_spread, 16)

            schedule(sp, body)
            for b in range(GB):
                sp.wait_ge(stored[b], 16 * NG)

        @block.tensor
        def _(pe):
            def product(dst, col, rows_hi, rows_lo, start, stop):
                for k in range(KC):
                    for w, r in ((wh, rows_hi), (wh, rows_lo), (wl, rows_hi)):
                        last = pe.matmul(dst, w[:, k, col * P:(col + 1) * P], r(k),
                                         start=(start and k == 0 and w is wh and r is rows_hi),
                                         stop=(stop and k == KC - 1 and w is wl))
                return last

            def unit_main(g, slot, b, half, bank, start_now=True):
                cols = slice(half * HALF, (half + 1) * HALF)
                for m in range(KC):
                    product(ps[bank][:, m], m, lambda k: hi[:, slot, b, k, cols],
                            lambda k: lo[:, slot, b, k, cols], True, False)

            def unit_rows(slot, b, half, bank, rows, signal):
                lanes = slice(b * ROWS, b * ROWS + PARTS * NC)
                for m in range(KC):
                    last = pe.matmul(ps[bank][:, m], rows(lanes, m),
                                     onehot[lanes, slot, half * HALF:(half + 1) * HALF],
                                     start=False, stop=True)
                last.then_inc(signal, 1)

            pe.wait_ge(const_ready, 5)
            pe.wait_ge(w_ready, 1)

            def body(g, slot, lap, main, mid_, prep):
                q, qs, ql = after(g, slot, lap, 1)
                p, pslot, plap = after(g, slot, lap, 2)

                def layer1(b, half):
                    u = b * NH + half
                    bank = (2 * UNITS * slot + u) % 3
                    pe.wait_ge(lo_ready, CH * g + KC * (b + 1))
                    if u < 3:
                        if some(UNITS * g - UNITS + (u + 2)):
                            pe.wait_ge(done, UNITS * g - UNITS + (u + 2))
                    else:
                        pe.wait_ge(l1_out, UNITS * g + (u - 2))
                    if u == 0:
                        pe.wait_ge(class_ready, g + 1)
                    unit_main(g, slot, b, half, bank)
                    unit_rows(slot, b, half, bank, lambda lanes, m: cut[lanes, :], l1_ps)

                def layer2(u):
                    bank = (2 * UNITS * slot + UNITS + u) % 3
                    if u < 3:
                        pe.wait_ge(l1_out, UNITS * g + (u + 2))
                    else:
                        pe.wait_ge(done, UNITS * g + (u - 2))
                    pe.wait_ge(lo2_ready, UNITS * g + u + 1)
                    unit_main(g, slot, u // NH, u % NH, bank)

                def layer2_rows(u):
                    bank = (2 * UNITS * slot + UNITS + u) % 3
                    unit_rows(slot, u // NH, u % NH, bank,
                              lambda lanes, m: l2w[lanes, m * P:(m + 1) * P], l2_ps)

                def class_sizes():
                    pe.wait_ge(fv_copied, q + 1)
                    pe.wait_ge(count_ready, q + 1)
                    if main:
                        if some(g):
                            pe.wait_ge(l2w_ready, g)
                    pe.matmul(pf_n, ones[:, :], count_r[:, qs], start=True, stop=True).then_inc(n_ready, 1)

                def times_q1():
                    pe.wait_ge(q1_ready, 3 * (q + 1))
                    for m in range(KC):
                        for k in range(KC):
                            last = pe.matmul(pf_q[:, m], wt[:, k, m * P:(m + 1) * P],
                                             q1[:, k].rearrange("p b c -> p (b c)"),
                                             start=(k == 0), stop=(k == KC - 1))
                    last.then_inc(wq1_ready, 1)

                def means():
                    if mid_:
                        pe.wait_ge(bv_ready, q + 1)
                    if some(g):
                        pe.wait_ge(l2w_ready, g)
                    for b in range(GB):
                        pe.wait_ge(lo_ready, CH * p + KC * (b + 1))
                        for half in range(NH):
                            cols = slice(half * HALF, (half + 1) * HALF)
                            for k in range(KC):
                                for part, t in enumerate((hi, lo)):
                                    first = b == 0 and k == 0 and part == 0
                                    end = b == GB - 1 and k == KC - 1 and part == 1
                                    last = pe.matmul(pf[0:R, cols], sums[:, b], t[:, pslot, b, k, cols],
                                                     start=first, stop=end)
                    last.then_inc(fv_ready, 1)

                def times_q2():
                    pe.wait_ge(q2_ready, KC * (g + 1))
                    if prep:
                        pe.wait_ge(fv_copied, p + 1)
                    for k in range(KC):
                        last = pe.matmul(pf_w, q2[:, k].rearrange("p b c -> p (b c)"), wt[:, k],
                                         start=(k == 0), stop=(k == KC - 1))
                    last.then_inc(wq2_ready, 1)

                if main:
                    layer1(0, 0)
                if mid_:
                    class_sizes()
                if main:
                    layer1(0, 1)
                    layer1(1, 0)
                if mid_:
                    times_q1()
                if main:
                    layer1(1, 1)
                if prep:
                    means()
                if main:
                    layer2(0)
                    times_q2()
                    layer2(1)
                    pe.wait_ge(l2w_ready, g + 1)
                    layer2_rows(0)
                    layer2_rows(1)
                    layer2(2)
                    layer2_rows(2)
                    layer2(3)
                    layer2_rows(3)

            schedule(pe, body)

        @block.scalar
        def _(act):
            act.wait_ge(loaded, 64)

            def body(g, slot, lap, main, mid_, prep):
                p, pslot, plap = after(g, slot, lap, 2)

                def root(b):
                    act.wait_ge(mv_ready, GB * p + b + 1)
                    act.activation(std[:, b], var[:, b], ACT.Sqrt).then_inc(std_ready, 1)

                def h_chunk(b, k):
                    if k == 0:
                        act.wait_ge(coef_ready, GB * p + b + 1)
                    if some(CH * p + KC * b + k - 1):
                        act.wait_ge(lo_ready, CH * p + KC * b + k - 1)
                    act.activation(hf[:, k], xs[:, pslot, b, k], ACT.Relu, bias=nbias[:, b, k:k + 1],
                                   scale=rstd[:, pslot, b, k:k + 1],
                                   accum_out=s_all[:, pslot, b, k:k + 1]).then_inc(h_ready, 1)

                def h_hi(b, k):
                    act.wait_ge(h_ready, CH * p + KC * b + k + 1)
                    if some(UNITS * (p - RING) + NH * (b + 1)):
                        act.wait_ge(l2_ps, UNITS * (p - RING) + NH * (b + 1))
                    act.activation(hi[:, pslot, b, k], hf[:, k], ACT.Copy).then_inc(hi_ready, 1)

                def means_copy():
                    act.wait_ge(fv_ready, p + 1)
                    if some(p):
                        act.wait_ge(t_ready, p)
                    act.activation(fv[:, 0:N], pf[0:R, :], ACT.Copy).then_inc(fv_copied, 1)

                def layer1_out(u):
                    b, half = u // NH, u % NH
                    bank = (2 * UNITS * slot + u) % 3
                    if u == 0:
                        act.wait_ge(bv_ready, g + 1)
                    act.wait_ge(l1_ps, UNITS * g + u + 1)
                    if some(UNITS * g + u - 1):
                        act.wait_ge(lo2_ready, UNITS * g + u - 1)
                    for m in range(KC):
                        last = act.activation(y1[:, u % 2, m], ps[bank][:, m], ACT.Relu,
                                              bias=bv[:, slot, m, b, 0:1], scale=1.0 / DEG,
                                              accum_out=acc[:, slot, m, b, half:half + 1])
                    if half == 0:
                        for m in range(KC):
                            last = act.activation(yu[:, slot, m, b], ps[bank][:, m, U0:U0 + NU], ACT.Relu,
                                                  bias=bv[:, slot, m, b, 4:5], scale=rdeg[:, slot, b, 4:5],
                                                  accum_out=yus[:, slot, m, b:b + 1])
                    last.then_inc(l1_out, 1)

                if prep:
                    root(0)
                    h_chunk(0, 0)
                    h_chunk(0, 1)
                    h_hi(0, 0)
                    h_hi(0, 1)
                if main:
                    layer1_out(0)
                    layer1_out(1)
                if prep:
                    root(1)
                    h_chunk(1, 0)
                    h_chunk(1, 1)
                if main:
                    layer1_out(2)
                if prep:
                    h_hi(1, 0)
                    h_hi(1, 1)
                if main:
                    layer1_out(3)
                if prep:
                    means_copy()

            schedule(act, body)

        @block.gpsimd
        def _(pool):
            def body(g, slot, lap, main, mid_, prep):
                q, qs, ql = after(g, slot, lap, 1)
                p, pslot, plap = after(g, slot, lap, 2)
                STEPS = 12

                def h_lo(b, k):
                    pool.wait_ge(hi_ready, CH * p + KC * b + k + 1)
                    pool.tensor_tensor(lo[:, pslot, b, k], hf[:, k], hi[:, pslot, b, k].bitcast(F32),
                                       ALU.subtract).then_inc(lo_ready, 1)

                def y_lo(u):
                    b, cols = u // NH, slice(u % NH * HALF, (u % NH + 1) * HALF)
                    pool.wait_ge(hi2_ready, UNITS * g + u + 1)
                    pool.tensor_tensor(lo[:, slot, b, :, cols], y1[:, u % 2],
                                       hi[:, slot, b, :, cols].bitcast(F32),
                                       ALU.subtract).then_inc(lo2_ready, 1)

                def class_sums():
                    step = [0]

                    def add(o, a, b_, needs=True, op=ALU.add):
                        ins = pool.tensor_tensor(o, a, b_, op).then_inc(pool_step, 1)
                        step[0] += 1
                        pool.wait_ge(pool_step, STEPS * q + step[0])

                    n, v, o = nd[:, qs, 0], v1[:, qs], p2[:, qs]
                    pool.wait_ge(bv_ready, q + 1)
                    for m in range(KC):
                        add(nv[:, m], n, v[:, m], op=ALU.mult)
                    e = nv[:, :, :, 1:5:2]
                    add(pt[:, 0], nv[:, :, :, 1], nv[:, :, :, 3])
                    add(pt[:, 2], nv[:, :, :, 5], nv[:, :, :, 7])
                    add(o[:, :, :, 0], pt[:, 0], pt[:, 2])
                    add(o[:, :, :, 1], pt[:, 0], pt[:, 2])
                    add(pt[:, 1], nv[:, :, :, 2], nv[:, :, :, 6])
                    for c in (4, 5, 7):
                        add(o[:, :, :, c], o[:, :, :, 0], pt[:, 1])
                    add(pt[:, 3], pt[:, 2], nv[:, :, :, 6])
                    add(o[:, :, :, 2], pt[:, 3], v[:, :, :, 2])
                    assert step[0] == STEPS, step
                    pool.tensor_tensor(pt[:, 4], nv[:, :, :, 3], pt[:, 1], ALU.add).then_inc(p2_ready, 1)
                    pool.tensor_tensor(pt[:, 5], nv[:, :, :, 1], v[:, :, :, 3], ALU.add).then_inc(p2_ready, 1)
                    pool.wait_ge(p2_ready, 4 * q + 2)
                    pool.tensor_tensor(o[:, :, :, 6], pt[:, 4], pt[:, 2], ALU.add).then_inc(p2_ready, 1)
                    pool.tensor_tensor(o[:, :, :, 3], pt[:, 5], pt[:, 3], ALU.add).then_inc(p2_ready, 1)

                if prep:
                    h_lo(0, 0)
                    h_lo(0, 1)
                if main:
                    y_lo(0)
                    y_lo(1)
                if prep:
                    h_lo(1, 0)
                if main:
                    y_lo(2)
                if prep:
                    h_lo(1, 1)
                if main:
                    y_lo(3)
                if mid_:
                    class_sums()

            schedule(pool, body)

        @block.vector
        def _(dve):
            dve.memset(sums[:].bitcast(F32), 0.0).then_inc(const_ready, 1)
            dve.memset(ones[:], 1.0).then_inc(const_ready, 1)
            dve.memset(q2[:], 0.0).then_inc(const_ready, 1)
            dve.wait_ge(const_ready, 3)
            for b in range(GB):
                last = dve.memset(sums[:, b, b * ROWS:(b + 1) * ROWS].bitcast(F32), 1.0)
            last.then_inc(const_ready, 1)
            dve.wait_ge(loaded, 64)
            dve.tensor_copy(cut[:], cs[0:R, C_CUT:C_CUT + P]).then_inc(const_ready, 1)
            dve.tensor_scalar(b2[:], b2[:], DEG, None, ALU.mult).then_inc(b2_ready, 1)
            dve.tensor_copy(wh[:], wt[:]).then_inc(w_hi, 1)
            dve.wait_ge(w_hi, 1)
            dve.tensor_tensor(wl[:], wt[:], wh[:].bitcast(F32), ALU.subtract).then_inc(w_ready, 1)

            def body(g, slot, lap, main, mid_, prep):
                q, qs, ql = after(g, slot, lap, 1)
                p, pslot, plap = after(g, slot, lap, 2)

                def stats(b):
                    dve.wait_ge(x_in[pslot][b], 16 * (plap + 1))
                    for k in range(KC):
                        for half in range(2):
                            dve.bn_stats(bn[:, k, half], xs[:, pslot, b, k, half * HALF:(half + 1) * HALF]
                                         ).then_inc(stats_done, 1)
                    hold(dve, stats_done, 4 * (GB * p + b + 1), b)
                    for k in range(KC):
                        dve.bn_aggr(mv[:, pslot, b, k], bn[:, k].rearrange("p a c -> p (a c)")
                                    ).then_inc(mv_done, 1)
                    dve.wait_ge(mv_done, 2 * (GB * p + b + 1))
                    dve.tensor_scalar(var[:, b], mv[:, pslot, b, :, 1], EPS, None, ALU.add
                                      ).then_inc(mv_ready, 1)

                def coefs(b):
                    at = 5 * (GB * p + b)
                    dve.wait_ge(std_ready, GB * p + b + 1)
                    dve.reciprocal(nw[:, 0], std[:, b]).then_inc(newton, 1)
                    dve.wait_ge(newton, at + 1)
                    dve.tensor_tensor(nw[:, 1], nw[:, 0], nw[:, 0], ALU.mult).then_inc(newton, 1)
                    dve.wait_ge(newton, at + 2)
                    dve.tensor_tensor(nw[:, 2], nw[:, 1], var[:, b], ALU.mult).then_inc(newton, 1)
                    dve.wait_ge(newton, at + 3)
                    dve.tensor_scalar(nw[:, 3], nw[:, 2], -0.5, 1.5, ALU.mult, ALU.add).then_inc(newton, 1)
                    dve.wait_ge(newton, at + 4)
                    dve.tensor_tensor(rstd[:, pslot, b], nw[:, 0], nw[:, 3], ALU.mult).then_inc(newton, 1)
                    dve.wait_ge(newton, at + 5)
                    dve.scalar_tensor_tensor(nbias[:, b], mv[:, pslot, b, :, 0], -1.0, rstd[:, pslot, b],
                                             ALU.mult, ALU.mult).then_inc(coef_ready, 1)

                def sum_neighbours(b):
                    dve.wait_ge(t_spread, 16 * GB * (q + 1))
                    if some(GB * q + b):
                        dve.wait_ge(st_done, GB * q + b)
                    for k in range(KC):
                        last = dve.scalar_tensor_tensor(junk[:, k], xs[:, qs, b, k], mv[:, qs, b, k, 0:1],
                                                        tmap[:, b], ALU.max, ALU.mult,
                                                        accum_out=s_max[:, b, k:k + 1])
                    last.then_inc(st_done, 1)

                def middle_a():
                    at = MID * q
                    dve.wait_ge(n_ready, q + 1)
                    dve.tensor_tensor(nd[:, qs].rearrange("p a b c -> p (a b c)"), pf_n,
                                      cs[:, C_BASE:C_BASE + 2 * GB * NC], ALU.add).then_inc(mid, 1)
                    dve.wait_ge(st_done, GB * (q + 1))
                    dve.scalar_tensor_tensor(s_t[:], mv[:, qs, :, :, 0], -float(TOPK), s_max[:],
                                             ALU.mult, ALU.add).then_inc(mid, 1)
                    for part, t in enumerate((hi, lo)):
                        dve.tensor_reduce(s_u[:, part], t[:, qs, :, :, U0:U0 + NU].bitcast(F32), AX.X, ALU.add
                                          ).then_inc(mid, 1)
                    dve.wait_ge(mid, at + 4)
                    dve.reciprocal(rdeg[:, qs], nd[:, qs, 1]).then_inc(mid, 1)
                    dve.tensor_tensor(s_t[:], s_t[:], rstd[:, qs], ALU.mult).then_inc(mid, 1)
                    dve.tensor_tensor(s_u[:, 2], s_u[:, 0], s_u[:, 1], ALU.add).then_inc(mid, 1)
                    dve.wait_ge(mid, at + 7)
                    dve.tensor_scalar(rdeg9[:, qs], rdeg[:, qs], DEG, None, ALU.mult).then_inc(mid, 1)
                    kb = "p b k -> p k b"
                    for src, cols in ((s_t[:], slice(0, NC, 4)), (s_u[:, 2], slice(2, NC, 4)),
                                      (s_all[:, qs], slice(1, NC, 2))):
                        n = NC // (cols.step)
                        dve.tensor_tensor(q1[:, :, :, cols],
                                          src.rearrange(kb).unsqueeze(3).to_broadcast([P, KC, GB, n]),
                                          rdeg[:, qs, :, cols].unsqueeze(1).to_broadcast([P, KC, GB, n]),
                                          ALU.mult).then_inc(q1_ready, 1)

                def middle_b():
                    dve.wait_ge(wq1_ready, q + 1)
                    for m in range(KC):
                        dve.tensor_scalar(bv[:, qs, m].rearrange("p b c -> p (b c)"), pf_q[:, m],
                                          b1[:, m:m + 1], None, ALU.add).then_inc(mid, 1)
                    dve.wait_ge(mid, MID * (q + 1))
                    dve.tensor_scalar(v1[:, qs], bv[:, qs], 0.0, None, ALU.max).then_inc(bv_ready, 1)

                def y_hi(u):
                    b, half = u // NH, u % NH
                    cols = slice(half * HALF, (half + 1) * HALF)
                    dve.wait_ge(l1_out, UNITS * g + u + 1)
                    if half == 0:
                        mine = y1[:, u % 2, :, U0:U0 + NU]
                        dve.tensor_reduce(wrong[:, :, b], mine, AX.X, ALU.add).then_inc(yu_fixed, 1)
                        dve.wait_ge(yu_fixed, 2 * (GB * g + b) + 1)
                        dve.tensor_scalar(mine, yu[:, slot, :, b], rdeg9[:, slot, b, 4:5], None, ALU.mult).then_inc(yu_fixed, 1)
                        dve.wait_ge(yu_fixed, 2 * (GB * g + b) + 2)
                    dve.tensor_copy(hi[:, slot, b, :, cols], y1[:, u % 2]).then_inc(hi2_ready, 1)

                def late_sums():
                    at = LATE * g
                    dve.wait_ge(p2_ready, 4 * (g + 1))
                    dve.tensor_tensor(snk[:, 0], acc[:, slot, :, :, 0], acc[:, slot, :, :, 1], ALU.add
                                      ).then_inc(late, 1)
                    dve.tensor_tensor(snk[:, 1], yus[:, slot], wrong[:], ALU.subtract).then_inc(late, 1)
                    o = p2[:, slot]
                    u_sum = yus[:, slot].unsqueeze(3).to_broadcast([P, KC, GB, 2])
                    dve.tensor_tensor(o[:, :, :, 2:NC:4], o[:, :, :, 2:NC:4], u_sum, ALU.add).then_inc(late, 1)
                    dve.wait_ge(late, at + 3)
                    dve.tensor_tensor(snk[:, 2], snk[:, 0], snk[:, 1], ALU.add).then_inc(late, 1)
                    dve.wait_ge(late, at + 4)
                    k_sum = snk[:, 2].unsqueeze(3).to_broadcast([P, KC, GB, 4])
                    dve.tensor_tensor(o[:, :, :, 1:NC:2], o[:, :, :, 1:NC:2], k_sum, ALU.add).then_inc(late, 1)
                    dve.wait_ge(late, at + LATE)
                    for k in range(KC):
                        dst = q2[:, k, :, 0:PARTS * NC].rearrange("p b (j c) -> p b j c", j=PARTS)
                        full = [P, GB, PARTS, NC]
                        dve.tensor_tensor(dst, o[:, k].unsqueeze(2).to_broadcast(full),
                                          rdeg9[:, slot].unsqueeze(2).to_broadcast(full), ALU.mult
                                          ).then_inc(q2_ready, 1)

                def layer2_weights():
                    dve.wait_ge(wq2_ready, g + 1)
                    dve.tensor_tensor(rx[:], pf_w, b2[:], ALU.add).then_inc(l2w_step, 1)
                    dve.wait_ge(l2w_step, 2 * g + 1)
                    dve.tensor_copy(rh[:], rx[:]).then_inc(l2w_step, 1)
                    dve.wait_ge(l2w_step, 2 * g + 2)
                    dve.scalar_tensor_tensor(l2w[:], rh[:].bitcast(F32), cs[0:R, C_NEG:C_NEG + 1],
                                             rx[:], ALU.mult, ALU.add).then_inc(l2w_ready, 1)

                def final(u):
                    b, half = u // NH, u % NH
                    cols = slice(half * HALF, (half + 1) * HALF)
                    bank = (2 * UNITS * slot + UNITS + u) % 3
                    dve.wait_ge(l2_ps, UNITS * g + u + 1)
                    if half == 0:
                        if some(16 * g):
                            dve.wait_ge(stored[b], 16 * g)
                    dve.scalar_tensor_tensor(ob[:, b, :, cols], ps[bank][:], 1.0 / DEG,
                                             xs[:, slot, b, :, cols], ALU.mult, ALU.add).then_inc(done, 1)

                at_k = TK * p

                def top_a():
                    dve.wait_ge(fv_copied, p + 1)
                    dve.memset(fv[:, N:N + PAD], -1.0).then_inc(topk, 1)
                    hold(dve, topk, at_k + 1, 2)
                    dve.max(top[:, 0], fv[:]).then_inc(topk, 1)
                    dve.tensor_scalar(code[:], fv[:, 0:N], 0.0, 2.0, ALU.is_equal, ALU.mult).then_inc(topk, 1)
                    dve.wait_ge(topk, at_k + 3)
                    dve.memset(top[:, 0, 1:8], -1.0).then_inc(topk, 1)
                    dve.tensor_scalar(code[:, U0:U0 + NU], code[:, U0:U0 + NU], 4.0, None, ALU.add
                                      ).then_inc(topk, 1)

                def top_b():
                    hold(dve, topk, at_k + 5, 3)
                    dve.match_replace(fv[:], top[:, 0], fv[:], -2.0).then_inc(topk, 1)
                    hold(dve, topk, at_k + 6, 4)
                    dve.max(top[:, 1], fv[:]).then_inc(topk, 1)

                def top_c():
                    hold(dve, topk, at_k + 7, 5)
                    dve.match_replace(fv[:], top[:, 1], fv[:], -3.0).then_inc(topk, 1)
                    if some(16 * p):
                        dve.wait_ge(t_saved, 16 * p)
                    dve.wait_ge(topk, at_k + 8)
                    dve.tensor_scalar(tr[:], fv[:, 0:N], -3.0, None, ALU.is_equal).then_inc(t_ready, 1)

                def classes():
                    dve.wait_ge(t_ready, p + 1)
                    dve.tensor_tensor(code[:], code[:], tr[:], ALU.add).then_inc(topk, 1)
                    dve.wait_ge(topk, at_k + TK)
                    dve.tensor_scalar(onehot[:, pslot], code[:], cs[0:R, C_WANT:C_WANT + 1], None,
                                      ALU.is_equal, ALU.add, accum_out=count[:, pslot:pslot + 1]
                                      ).then_inc(class_ready, 1)
                    dve.wait_ge(class_ready, p + 1)
                    dve.tensor_scalar(count_r[:, pslot], cs[0:R, C_PICK:C_PICK + 2 * GB * NC],
                                      count[:, pslot:pslot + 1], None, ALU.mult).then_inc(count_ready, 1)

                if prep:
                    stats(0)
                if mid_:
                    sum_neighbours(0)
                if prep:
                    coefs(0)
                if main:
                    y_hi(0)
                if mid_:
                    sum_neighbours(1)
                    middle_a()
                if main:
                    y_hi(1)
                if prep:
                    stats(1)
                    coefs(1)
                if main:
                    y_hi(2)
                if mid_:
                    middle_b()
                if main:
                    y_hi(3)
                    late_sums()
                if prep:
                    top_a()
                if main:
                    layer2_weights()
                if prep:
                    top_b()
                if main:
                    final(0)
                if prep:
                    top_c()
                if main:
                    final(1)
                if prep:
                    classes()
                if main:
                    final(2)
                    final(3)

            schedule(dve, body)


_OUT = (B, S, N)


def kernel(x, adj, L0_gnn_b1, L0_gnn_b2):
    import numpy as np
    import concourse.bacc as bacc
    from concourse.bass_utils import run_bass_kernel_spmd

    nc = bacc.Bacc("TRN2", target_bir_lowering=False, num_devices=1, dynamic_dma_scratch_size=1024)
    arrays = {
        "x_dram": np.ascontiguousarray(x),
        "adj_t_dram": np.ascontiguousarray(np.asarray(adj).T),
        "b1_dram": np.ascontiguousarray(np.asarray(L0_gnn_b1).reshape(KC, P).T),
        "b2_dram": np.ascontiguousarray(np.asarray(L0_gnn_b2).reshape(1, S)),
        "consts_dram": node_class_constants(),
    }
    args = [nc.dram_tensor(name, a.shape, mybir.dt.from_np(a.dtype), kind="ExternalInput").ap()
            for name, a in arrays.items()]
    out = nc.dram_tensor("out_dram", _OUT, F32, kind="ExternalOutput").ap()
    gnn_kernel(nc, *args, out)
    r = run_bass_kernel_spmd(nc, [arrays], core_ids=[0])
    return r.results[0]["out_dram"]
```

```python
import concourse.bass as bass
from concourse import mybir
from concourse.alu_op_type import AluOpType as ALU
from contextlib import ExitStack

ACT = mybir.ActivationFunctionType
AX = mybir.AxisListType
F32 = mybir.dt.float32
F32R = mybir.dt.float32r
BF16 = mybir.dt.bfloat16

B, S, N = 32, 256, 1024
P = 128
KC = S // P
HALF = 512
NH = N // HALF
GB = 2
NG = B // GB
RING = 3
CH = GB * KC
UNITS = GB * NH
TOPK = 8
NC = 8
ROWS = 32
R = GB * ROWS
PARTS = 2
NU = TOPK
U0 = 1
DEG = float(TOPK + 1)
EPS = 1e-5
BIG = 2.0 ** 100
PAD = 8


def node_class_constants():
    import numpy as np

    lanes = np.arange(R)
    cls, part = lanes % NC, (lanes % ROWS) // NC
    want = np.zeros((P, 2), np.float32)
    want[:R, 0] = cls
    want[:R, 1] = np.where(part == 1, -1, 0)
    const = np.array([DEG, N, DEG, N + 1, DEG, N, 0, N], np.float32)
    coef = np.zeros((NC, NC), np.float32)
    coef[[2, 6], 1] = -1
    coef[[2, 3], 3] = -1
    coef[[2, 6], 4] = 1
    coef[[2, 3, 6, 7, 4, 5], 6] = 1
    pick = np.zeros((P, 2, GB, NC), np.float32)
    for p in range(R):
        if part[p] == 0:
            b = p // ROWS
            pick[p, 0, b, cls[p]] = 1
            pick[p, 1, b, :] = coef[cls[p]]
    base = np.zeros((P, 2, GB, NC), np.float32)
    base[:, 1] = const
    cut = np.zeros((P, P), np.float32)
    cut[:R][(part == 0) & (cls % 4 != 0)] = -BIG
    return np.concatenate([want, pick.reshape(P, -1), base.reshape(P, -1), cut], 1)


MID = 10
LATE = 5
TK = 9

C_WANT, C_NEG, C_PICK = 0, 1, 2
C_BASE = C_PICK + 2 * GB * NC
C_CUT = C_BASE + 2 * GB * NC
C_ALL = C_CUT + P


def gnn_kernel(nc, x, adj_t, bias1, bias2, consts, out):
    x_v = x.rearrange("b (k p) n -> b p k n", p=P)
    out_v = out.rearrange("b (k p) n -> b p k n", p=P)
    t_rows = nc.dram_tensor("t_rows", (B, N), BF16, kind="Internal").ap()

    with ExitStack() as ctx:
        def sb(name, shape, dt=F32):
            return ctx.enter_context(nc.sbuf_tensor(name, shape, dt))

        def sem(name):
            return ctx.enter_context(nc.semaphore(name))

        xs = sb("xs", [P, RING, GB, KC, N])
        hi = sb("hi", [P, RING, GB, KC, N], F32R)
        lo = sb("lo", [P, RING, GB, KC, N], F32R)
        hf = sb("hf", [P, KC, N])
        y1 = sb("y1", [P, 2, KC, HALF])
        ob = sb("ob", [P, GB, KC, N])
        wt = sb("wt", [P, KC, S])
        wh = sb("wh", [P, KC, S], F32R)
        wl = sb("wl", [P, KC, S], F32R)
        cs = sb("cs", [P, C_ALL])
        b1 = sb("b1", [P, KC])
        b2 = sb("b2", [R, S])
        cut = sb("cut", [R, P], F32R)
        sums = sb("sums", [P, R], F32R)
        spare = sb("spare", [P, 8])
        ones = sb("ones", [R, P])
        fv = sb("fv", [R, N + PAD])
        top = sb("top", [R, 2, 8])
        code = sb("code", [R, N], BF16)
        tr = sb("tr", [R, N], BF16)
        onehot = sb("onehot", [R, RING, N], F32R)
        count = sb("count", [R, RING])
        count_r = sb("count_r", [R, RING, 2 * GB * NC])
        tmap = sb("tmap", [P, GB, N], BF16)
        junk = sb("junk", [P, 2, N], BF16)
        bn = sb("bn", [P, KC, 2, 6])
        mv = sb("mv", [P, RING, GB, KC, 2])
        var = sb("var", [P, GB, KC])
        std = sb("std", [P, GB, KC])
        nw = sb("nw", [P, 4, KC])
        rstd = sb("rstd", [P, RING, GB, KC])
        nbias = sb("nbias", [P, GB, KC])
        s_all = sb("s_all", [P, RING, GB, KC])
        s_max = sb("s_max", [P, GB, KC])
        s_t = sb("s_t", [P, GB, KC])
        s_u = sb("s_u", [P, 3, GB, KC])
        nd = sb("nd", [P, RING, 2, GB, NC])
        rdeg = sb("rdeg", [P, RING, GB, NC])
        rdeg9 = sb("rdeg9", [P, RING, GB, NC])
        q1 = sb("q1", [P, KC, GB, NC])
        bv = sb("bv", [P, RING, KC, GB, NC])
        v1 = sb("v1", [P, RING, KC, GB, NC])
        nv = sb("nv", [P, KC, GB, NC])
        pt = sb("pt", [P, 6, KC, GB])
        p2 = sb("p2", [P, RING, KC, GB, NC])
        acc = sb("acc", [P, RING, KC, GB, NH + 2])
        yu = sb("yu", [P, GB, KC, NU])
        snk = sb("snk", [P, 3, KC, GB])
        q2 = sb("q2", [P, KC, GB, ROWS])
        rx = sb("rx", [R, S])
        rh = sb("rh", [R, S], F32R)
        l2w = sb("l2w", [R, S], F32R)

        ps = [ctx.enter_context(nc.psum_tensor(f"ps{i}", [P, KC, HALF], F32)) for i in range(3)]
        pf = ctx.enter_context(nc.psum_tensor("pf", [P, N], F32))
        pf_n = pf[:, 0:2 * GB * NC]
        pf_q = pf[:, 64:64 + KC * GB * NC].rearrange("p (m c) -> p m c", m=KC)

        def bank_of(slot, unit):
            return (2 * UNITS * slot + unit) % 3

        def q2_bank(slot):
            return ps[bank_of(slot, UNITS + 2)][0:R, 0, 0:S]

        x_in = [[sem(f"x_in{s}{b}") for b in range(GB)] for s in range(RING)]
        loaded = sem("loaded")
        const_ready = sem("const_ready")
        b2_ready = sem("b2_ready")
        w_hi = sem("w_hi")
        w_ready = sem("w_ready")
        stats_done = sem("stats_done")
        mv_done = sem("mv_done")
        mv_ready = sem("mv_ready")
        std_ready = sem("std_ready")
        newton = sem("newton")
        coef_ready = sem("coef_ready")
        h_ready = sem("h_ready")
        hi_ready = sem("hi_ready")
        lo_ready = sem("lo_ready")
        fv_ready = sem("fv_ready")
        fv_copied = sem("fv_copied")
        topk = sem("topk")
        t_ready = sem("t_ready")
        class_ready = sem("class_ready")
        count_ready = sem("count_ready")
        t_saved = sem("t_saved")
        t_spread = sem("t_spread")
        st_done = sem("st_done")
        n_ready = sem("n_ready")
        mid = sem("mid")
        q1_ready = sem("q1_ready")
        wq1_ready = sem("wq1_ready")
        bv_ready = sem("bv_ready")
        pool_step = sem("pool_step")
        p2_ready = sem("p2_ready")
        l1_ps = sem("l1_ps")
        l1_out = sem("l1_out")
        yu_scaled = sem("yu_scaled")
        hi2_ready = sem("hi2_ready")
        lo2_ready = sem("lo2_ready")
        late = sem("late")
        q2_ready = sem("q2_ready")
        wq2_ready = sem("wq2_ready")
        l2w_step = sem("l2w_step")
        l2w_ready = sem("l2w_ready")
        l2_ps = sem("l2_ps")
        done = sem("done")
        stored = [sem(f"stored{b}") for b in range(GB)]

        def some(value):
            return not isinstance(value, int) or value > 0

        def hold(dve, s, value, column):
            dve.wait_ge(s, value)
            dve.memset(spare[:, column:column + 1], 0.0)

        def after(g, slot, lap, d):
            return g + d, (slot + d) % RING, lap + (slot + d) // RING

        def schedule(eng, body):
            body(-2, 1, -1, False, False, True)
            body(-1, 2, -1, False, True, True)
            body(0, 0, 0, True, True, True)
            laps = (NG - 3) // RING
            with eng.Fori(0, laps) as i:
                for j in range(RING):
                    g, slot = 3 * i + (1 + j), (1 + j) % RING
                    body(g, slot, i + (1 + j) // RING, True, True, True)
            for g in range(1 + RING * laps, NG):
                body(g, g % RING, g // RING, True, g + 1 < NG, g + 2 < NG)

        block = ctx.enter_context(nc.Block())

        @block.sync
        def _(sp):
            for dst, src in ((wt[:], adj_t.rearrange("(k p) o -> p k o", p=P)), (cs[:], consts),
                             (b1[:], bias1), (b2[:], bias2.to_broadcast([R, S]))):
                sp.dma_start(dst, src).then_inc(loaded, 16)

            def load(g, slot, b):
                sp.dma_start(xs[:, slot, b], x_v[g * GB + b]).then_inc(x_in[slot][b], 16)

            for g in range(RING):
                for b in range(GB):
                    load(g, g, b)

            def body(g, slot, lap, main, mid_, prep):
                def store(b):
                    sp.wait_ge(done, UNITS * g + NH * (b + 1))
                    sp.dma_start(out_v[g * GB + b], ob[:, b]).then_inc(stored[b], 16)

                if mid_:
                    q = g + 1
                    sp.wait_ge(t_ready, q + 1)
                    sp.dma_start(t_rows[bass.ds(q * GB, GB)], tr[0:R:ROWS, :]).then_inc(t_saved, 16)
                    sp.wait_ge(t_saved, 16 * (q + 1))
                    if some(GB * q):
                        sp.wait_ge(st_done, GB * q)
                    for b in range(GB):
                        sp.dma_start(tmap[:, b], t_rows[bass.ds(q * GB + b, 1)].to_broadcast([P, N])
                                     ).then_inc(t_spread, 16)
                if main:
                    for b in range(GB):
                        store(b)
                        if not isinstance(g, int) or g + RING < NG:
                            load(g + RING, slot, b)

            schedule(sp, body)
            for b in range(GB):
                sp.wait_ge(stored[b], 16 * NG)

        @block.tensor
        def _(pe):
            def product(dst, col, rows_hi, rows_lo, start, stop):
                for k in range(KC):
                    for w, r in ((wh, rows_hi), (wh, rows_lo), (wl, rows_hi)):
                        last = pe.matmul(dst, w[:, k, col * P:(col + 1) * P], r(k),
                                         start=(start and k == 0 and w is wh and r is rows_hi),
                                         stop=(stop and k == KC - 1 and w is wl))
                return last

            def unit_main(g, slot, b, half, bank, start_now=True):
                cols = slice(half * HALF, (half + 1) * HALF)
                for m in range(KC):
                    product(ps[bank][:, m], m, lambda k: hi[:, slot, b, k, cols],
                            lambda k: lo[:, slot, b, k, cols], True, False)

            def unit_rows(slot, b, half, bank, rows, signal):
                lanes = slice(b * ROWS, b * ROWS + PARTS * NC)
                for m in range(KC):
                    last = pe.matmul(ps[bank][:, m], rows(lanes, m),
                                     onehot[lanes, slot, half * HALF:(half + 1) * HALF],
                                     start=False, stop=True)
                last.then_inc(signal, 1)

            pe.wait_ge(const_ready, 4)
            pe.wait_ge(w_ready, 1)

            def body(g, slot, lap, main, mid_, prep):
                q, qs, ql = after(g, slot, lap, 1)
                p, pslot, plap = after(g, slot, lap, 2)

                def layer1(b, half):
                    u = b * NH + half
                    bank = bank_of(slot, u)
                    pe.wait_ge(lo_ready, CH * g + KC * (b + 1))
                    if u < 3:
                        if some(UNITS * g - UNITS + (u + 2)):
                            pe.wait_ge(done, UNITS * g - UNITS + (u + 2))
                    else:
                        pe.wait_ge(l1_out, UNITS * g + (u - 2))
                    if u == 0:
                        pe.wait_ge(class_ready, g + 1)
                    unit_main(g, slot, b, half, bank)
                    unit_rows(slot, b, half, bank, lambda lanes, m: cut[lanes, :], l1_ps)

                def layer2(u):
                    bank = bank_of(slot, UNITS + u)
                    if u < 3:
                        pe.wait_ge(l1_out, UNITS * g + (u + 2))
                    else:
                        pe.wait_ge(done, UNITS * g + (u - 2))
                    pe.wait_ge(lo2_ready, UNITS * g + u + 1)
                    unit_main(g, slot, u // NH, u % NH, bank)

                def layer2_rows(u):
                    bank = bank_of(slot, UNITS + u)
                    unit_rows(slot, u // NH, u % NH, bank,
                              lambda lanes, m: l2w[lanes, m * P:(m + 1) * P], l2_ps)

                def class_sizes():
                    if prep:
                        pe.wait_ge(fv_copied, GB * p + 1)
                    pe.wait_ge(count_ready, q + 1)
                    pe.matmul(pf_n, ones[:, :], count_r[:, qs], start=True, stop=True).then_inc(n_ready, 1)

                def times_q1():
                    pe.wait_ge(q1_ready, 3 * (q + 1))
                    for m in range(KC):
                        for k in range(KC):
                            last = pe.matmul(pf_q[:, m], wt[:, k, m * P:(m + 1) * P],
                                             q1[:, k].rearrange("p b c -> p (b c)"),
                                             start=(k == 0), stop=(k == KC - 1))
                    last.then_inc(wq1_ready, 1)

                def means(b):
                    if b == 0:
                        if some(g + 1):
                            pe.wait_ge(bv_ready, g + 1)
                        if some(GB * (g + 2)):
                            pe.wait_ge(fv_copied, GB * (g + 2))
                    elif mid_:
                        pe.wait_ge(bv_ready, q + 1)
                    else:
                        pe.wait_ge(fv_copied, GB * p + 1)
                    pe.wait_ge(lo_ready, CH * p + KC * (b + 1))
                    for half in range(NH):
                        cols = slice(half * HALF, (half + 1) * HALF)
                        for k in range(KC):
                            for part, t in enumerate((hi, lo)):
                                last = pe.matmul(pf[0:R, cols], sums[:], t[:, pslot, b, k, cols],
                                                 start=(k == 0 and part == 0),
                                                 stop=(k == KC - 1 and part == 1))
                    last.then_inc(fv_ready, 1)

                def times_q2():
                    pe.wait_ge(q2_ready, KC * (g + 1))
                    pe.wait_ge(l1_out, UNITS * (g + 1))
                    for k in range(KC):
                        last = pe.matmul(q2_bank(slot), q2[:, k].rearrange("p b c -> p (b c)"), wt[:, k],
                                         start=(k == 0), stop=(k == KC - 1))
                    last.then_inc(wq2_ready, 1)

                if main:
                    for u in range(UNITS):
                        layer1(u // NH, u % NH)
                    layer2(0)
                    layer2(1)
                    times_q2()
                if prep:
                    means(0)
                if main:
                    pe.wait_ge(l2w_ready, g + 1)
                    layer2_rows(0)
                    layer2_rows(1)
                    layer2(2)
                if mid_:
                    class_sizes()
                if main:
                    layer2_rows(2)
                    layer2(3)
                if mid_:
                    times_q1()
                if main:
                    layer2_rows(3)
                if prep:
                    means(1)

            schedule(pe, body)

        @block.scalar
        def _(act):
            act.wait_ge(loaded, 64)

            def body(g, slot, lap, main, mid_, prep):
                p, pslot, plap = after(g, slot, lap, 2)

                def root(b):
                    act.wait_ge(mv_ready, GB * p + b + 1)
                    act.activation(std[:, b], var[:, b], ACT.Sqrt).then_inc(std_ready, 1)

                def h_chunk(b, k):
                    if k == 0:
                        act.wait_ge(coef_ready, GB * p + b + 1)
                    if some(CH * p + KC * b + k - 1):
                        act.wait_ge(lo_ready, CH * p + KC * b + k - 1)
                    act.activation(hf[:, k], xs[:, pslot, b, k], ACT.Relu, bias=nbias[:, b, k:k + 1],
                                   scale=rstd[:, pslot, b, k:k + 1],
                                   accum_out=s_all[:, pslot, b, k:k + 1]).then_inc(h_ready, 1)

                def h_hi(b, k):
                    act.wait_ge(h_ready, CH * p + KC * b + k + 1)
                    if some(UNITS * (p - RING) + NH * (b + 1)):
                        act.wait_ge(l2_ps, UNITS * (p - RING) + NH * (b + 1))
                    act.activation(hi[:, pslot, b, k], hf[:, k], ACT.Copy).then_inc(hi_ready, 1)

                def means_copy(b):
                    act.wait_ge(fv_ready, GB * p + b + 1)
                    if b == 0 and some(p):
                        act.wait_ge(t_ready, p)
                    lanes = slice(b * ROWS, (b + 1) * ROWS)
                    act.activation(fv[lanes, 0:N], pf[lanes, :], ACT.Copy).then_inc(fv_copied, 1)

                def layer1_out(u):
                    b, half = u // NH, u % NH
                    bank = bank_of(slot, u)
                    if u == 0:
                        act.wait_ge(bv_ready, g + 1)
                    act.wait_ge(l1_ps, UNITS * g + u + 1)
                    if some(UNITS * g + u - 1):
                        act.wait_ge(lo2_ready, UNITS * g + u - 1)
                    bias = bv[:, slot, :, b]
                    first = U0 + NU if half == 0 else 0
                    for m in range(KC):
                        last = act.activation(y1[:, u % 2, m, first:], ps[bank][:, m, first:], ACT.Relu,
                                              bias=bias[:, m, 0:1], scale=1.0 / DEG,
                                              accum_out=acc[:, slot, m, b, half:half + 1])
                    if half == 0:
                        for m in range(KC):
                            act.activation(y1[:, u % 2, m, 0:U0], ps[bank][:, m, 0:U0], ACT.Relu,
                                           bias=bias[:, m, 0:1], scale=1.0 / DEG,
                                           accum_out=acc[:, slot, m, b, 2:3])
                            last = act.activation(yu[:, b, m], ps[bank][:, m, U0:U0 + NU], ACT.Relu,
                                                  bias=bias[:, m, 4:5], scale=rdeg[:, slot, b, 4:5],
                                                  accum_out=acc[:, slot, m, b, 3:4])
                    last.then_inc(l1_out, 1)
                    act.wait_ge(l1_out, UNITS * g + u + 1)
                    if half == 0:
                        act.activation(y1[:, u % 2, :, U0:U0 + NU], yu[:, b], ACT.Copy,
                                       scale=rdeg9[:, slot, b, 4:5]).then_inc(yu_scaled, 1)
                        act.wait_ge(yu_scaled, GB * g + b + 1)
                    act.activation(hi[:, slot, b, :, half * HALF:(half + 1) * HALF], y1[:, u % 2],
                                   ACT.Copy).then_inc(hi2_ready, 1)

                if prep:
                    root(0)
                if main:
                    layer1_out(0)
                if prep:
                    h_chunk(0, 0)
                    h_chunk(0, 1)
                if main:
                    layer1_out(1)
                if prep:
                    h_hi(0, 0)
                    h_hi(0, 1)
                if main:
                    layer1_out(2)
                    layer1_out(3)
                if prep:
                    root(1)
                    h_chunk(1, 0)
                    h_chunk(1, 1)
                    means_copy(0)
                    h_hi(1, 0)
                    h_hi(1, 1)
                    means_copy(1)

            schedule(act, body)

        @block.gpsimd
        def _(pool):
            def body(g, slot, lap, main, mid_, prep):
                p, pslot, plap = after(g, slot, lap, 2)
                STEPS = 12

                def h_lo(b, k):
                    pool.wait_ge(hi_ready, CH * p + KC * b + k + 1)
                    pool.tensor_tensor(lo[:, pslot, b, k], hf[:, k], hi[:, pslot, b, k].bitcast(F32),
                                       ALU.subtract).then_inc(lo_ready, 1)

                def y_lo(u):
                    b, cols = u // NH, slice(u % NH * HALF, (u % NH + 1) * HALF)
                    pool.wait_ge(hi2_ready, UNITS * g + u + 1)
                    pool.tensor_tensor(lo[:, slot, b, :, cols], y1[:, u % 2],
                                       hi[:, slot, b, :, cols].bitcast(F32),
                                       ALU.subtract).then_inc(lo2_ready, 1)

                def class_sums():
                    step = [0]

                    def add(o, a, b_, needs=True, op=ALU.add):
                        ins = pool.tensor_tensor(o, a, b_, op).then_inc(pool_step, 1)
                        step[0] += 1
                        pool.wait_ge(pool_step, STEPS * g + step[0])

                    n, v, o = nd[:, slot, 0], v1[:, slot], p2[:, slot]
                    pool.wait_ge(bv_ready, g + 1)
                    for m in range(KC):
                        add(nv[:, m], n, v[:, m], op=ALU.mult)
                    e = nv[:, :, :, 1:5:2]
                    add(pt[:, 0], nv[:, :, :, 1], nv[:, :, :, 3])
                    add(pt[:, 2], nv[:, :, :, 5], nv[:, :, :, 7])
                    add(o[:, :, :, 0], pt[:, 0], pt[:, 2])
                    add(o[:, :, :, 1], pt[:, 0], pt[:, 2])
                    add(pt[:, 1], nv[:, :, :, 2], nv[:, :, :, 6])
                    for c in (4, 5, 7):
                        add(o[:, :, :, c], o[:, :, :, 0], pt[:, 1])
                    add(pt[:, 3], pt[:, 2], nv[:, :, :, 6])
                    add(o[:, :, :, 2], pt[:, 3], v[:, :, :, 2])
                    assert step[0] == STEPS, step
                    pool.tensor_tensor(pt[:, 4], nv[:, :, :, 3], pt[:, 1], ALU.add).then_inc(p2_ready, 1)
                    pool.tensor_tensor(pt[:, 5], nv[:, :, :, 1], v[:, :, :, 3], ALU.add).then_inc(p2_ready, 1)
                    pool.wait_ge(p2_ready, 4 * g + 2)
                    pool.tensor_tensor(o[:, :, :, 6], pt[:, 4], pt[:, 2], ALU.add).then_inc(p2_ready, 1)
                    pool.tensor_tensor(o[:, :, :, 3], pt[:, 5], pt[:, 3], ALU.add).then_inc(p2_ready, 1)

                if main:
                    class_sums()
                    y_lo(0)
                    y_lo(1)
                if prep:
                    h_lo(0, 0)
                    h_lo(0, 1)
                if main:
                    y_lo(2)
                    y_lo(3)
                if prep:
                    h_lo(1, 0)
                    h_lo(1, 1)

            schedule(pool, body)

        @block.vector
        def _(dve):
            dve.memset(sums[:].bitcast(F32), 1.0).then_inc(const_ready, 1)
            dve.memset(ones[:], 1.0).then_inc(const_ready, 1)
            dve.memset(q2[:], 0.0).then_inc(const_ready, 1)
            dve.wait_ge(loaded, 64)
            dve.tensor_copy(cut[:], cs[0:R, C_CUT:C_CUT + P]).then_inc(const_ready, 1)
            dve.tensor_scalar(b2[:], b2[:], DEG, None, ALU.mult).then_inc(b2_ready, 1)
            dve.tensor_copy(wh[:], wt[:]).then_inc(w_hi, 1)
            dve.wait_ge(w_hi, 1)
            dve.tensor_tensor(wl[:], wt[:], wh[:].bitcast(F32), ALU.subtract).then_inc(w_ready, 1)

            def body(g, slot, lap, main, mid_, prep):
                q, qs, ql = after(g, slot, lap, 1)
                p, pslot, plap = after(g, slot, lap, 2)

                def stats(b):
                    dve.wait_ge(x_in[pslot][b], 16 * (plap + 1))
                    for k in range(KC):
                        for half in range(2):
                            dve.bn_stats(bn[:, k, half], xs[:, pslot, b, k, half * HALF:(half + 1) * HALF]
                                         ).then_inc(stats_done, 1)
                    hold(dve, stats_done, 4 * (GB * p + b + 1), b)
                    for k in range(KC):
                        dve.bn_aggr(mv[:, pslot, b, k], bn[:, k].rearrange("p a c -> p (a c)")
                                    ).then_inc(mv_done, 1)
                    dve.wait_ge(mv_done, 2 * (GB * p + b + 1))
                    dve.tensor_scalar(var[:, b], mv[:, pslot, b, :, 1], EPS, None, ALU.add
                                      ).then_inc(mv_ready, 1)

                def coefs(b):
                    at = 5 * (GB * p + b)
                    dve.wait_ge(std_ready, GB * p + b + 1)
                    dve.reciprocal(nw[:, 0], std[:, b]).then_inc(newton, 1)
                    dve.wait_ge(newton, at + 1)
                    dve.tensor_tensor(nw[:, 1], nw[:, 0], nw[:, 0], ALU.mult).then_inc(newton, 1)
                    dve.wait_ge(newton, at + 2)
                    dve.tensor_tensor(nw[:, 2], nw[:, 1], var[:, b], ALU.mult).then_inc(newton, 1)
                    dve.wait_ge(newton, at + 3)
                    dve.tensor_scalar(nw[:, 3], nw[:, 2], -0.5, 1.5, ALU.mult, ALU.add).then_inc(newton, 1)
                    dve.wait_ge(newton, at + 4)
                    dve.tensor_tensor(rstd[:, pslot, b], nw[:, 0], nw[:, 3], ALU.mult).then_inc(newton, 1)
                    dve.wait_ge(newton, at + 5)
                    dve.scalar_tensor_tensor(nbias[:, b], mv[:, pslot, b, :, 0], -1.0, rstd[:, pslot, b],
                                             ALU.mult, ALU.mult).then_inc(coef_ready, 1)

                def sum_neighbours(b):
                    dve.wait_ge(t_spread, 16 * GB * (q + 1))
                    if some(GB * q + b):
                        dve.wait_ge(st_done, GB * q + b)
                    for k in range(KC):
                        last = dve.scalar_tensor_tensor(junk[:, k], xs[:, qs, b, k], mv[:, qs, b, k, 0:1],
                                                        tmap[:, b], ALU.max, ALU.mult,
                                                        accum_out=s_max[:, b, k:k + 1])
                    last.then_inc(st_done, 1)

                def middle_a():
                    at = MID * q
                    dve.wait_ge(n_ready, q + 1)
                    dve.tensor_tensor(nd[:, qs].rearrange("p a b c -> p (a b c)"), pf_n,
                                      cs[:, C_BASE:C_BASE + 2 * GB * NC], ALU.add).then_inc(mid, 1)
                    dve.wait_ge(st_done, GB * (q + 1))
                    dve.scalar_tensor_tensor(s_t[:], mv[:, qs, :, :, 0], -float(TOPK), s_max[:],
                                             ALU.mult, ALU.add).then_inc(mid, 1)
                    for part, t in enumerate((hi, lo)):
                        dve.tensor_reduce(s_u[:, part], t[:, qs, :, :, U0:U0 + NU].bitcast(F32), AX.X, ALU.add
                                          ).then_inc(mid, 1)
                    dve.wait_ge(mid, at + 4)
                    dve.reciprocal(rdeg[:, qs], nd[:, qs, 1]).then_inc(mid, 1)
                    dve.tensor_tensor(s_t[:], s_t[:], rstd[:, qs], ALU.mult).then_inc(mid, 1)
                    dve.tensor_tensor(s_u[:, 2], s_u[:, 0], s_u[:, 1], ALU.add).then_inc(mid, 1)
                    dve.wait_ge(mid, at + 7)
                    dve.tensor_scalar(rdeg9[:, qs], rdeg[:, qs], DEG, None, ALU.mult).then_inc(mid, 1)
                    kb = "p b k -> p k b"
                    for src, cols in ((s_t[:], slice(0, NC, 4)), (s_u[:, 2], slice(2, NC, 4)),
                                      (s_all[:, qs], slice(1, NC, 2))):
                        n = NC // (cols.step)
                        dve.tensor_tensor(q1[:, :, :, cols],
                                          src.rearrange(kb).unsqueeze(3).to_broadcast([P, KC, GB, n]),
                                          rdeg[:, qs, :, cols].unsqueeze(1).to_broadcast([P, KC, GB, n]),
                                          ALU.mult).then_inc(q1_ready, 1)

                def middle_b():
                    dve.wait_ge(wq1_ready, q + 1)
                    for m in range(KC):
                        dve.tensor_scalar(bv[:, qs, m].rearrange("p b c -> p (b c)"), pf_q[:, m],
                                          b1[:, m:m + 1], None, ALU.add).then_inc(mid, 1)
                    dve.wait_ge(mid, MID * (q + 1))
                    dve.tensor_scalar(v1[:, qs], bv[:, qs], 0.0, None, ALU.max).then_inc(bv_ready, 1)

                def late_sums():
                    at = LATE * g
                    dve.wait_ge(p2_ready, 4 * (g + 1))
                    dve.wait_ge(l1_out, UNITS * (g + 1))
                    dve.tensor_tensor(snk[:, 0], acc[:, slot, :, :, 0], acc[:, slot, :, :, 1], ALU.add
                                      ).then_inc(late, 1)
                    dve.tensor_tensor(snk[:, 1], acc[:, slot, :, :, 2], acc[:, slot, :, :, 3], ALU.add
                                      ).then_inc(late, 1)
                    o = p2[:, slot]
                    u_sum = acc[:, slot, :, :, 3].unsqueeze(3).to_broadcast([P, KC, GB, 2])
                    dve.tensor_tensor(o[:, :, :, 2:NC:4], o[:, :, :, 2:NC:4], u_sum, ALU.add).then_inc(late, 1)
                    dve.wait_ge(late, at + 3)
                    dve.tensor_tensor(snk[:, 2], snk[:, 0], snk[:, 1], ALU.add).then_inc(late, 1)
                    dve.wait_ge(late, at + 4)
                    k_sum = snk[:, 2].unsqueeze(3).to_broadcast([P, KC, GB, 4])
                    dve.tensor_tensor(o[:, :, :, 1:NC:2], o[:, :, :, 1:NC:2], k_sum, ALU.add).then_inc(late, 1)
                    dve.wait_ge(late, at + LATE)
                    for k in range(KC):
                        dst = q2[:, k, :, 0:PARTS * NC].rearrange("p b (j c) -> p b j c", j=PARTS)
                        full = [P, GB, PARTS, NC]
                        dve.tensor_tensor(dst, o[:, k].unsqueeze(2).to_broadcast(full),
                                          rdeg9[:, slot].unsqueeze(2).to_broadcast(full), ALU.mult
                                          ).then_inc(q2_ready, 1)

                def layer2_weights():
                    dve.wait_ge(wq2_ready, g + 1)
                    dve.tensor_tensor(rx[:], q2_bank(slot), b2[:], ALU.add).then_inc(l2w_step, 1)
                    dve.wait_ge(l2w_step, 2 * g + 1)
                    dve.tensor_copy(rh[:], rx[:]).then_inc(l2w_step, 1)
                    dve.wait_ge(l2w_step, 2 * g + 2)
                    dve.scalar_tensor_tensor(l2w[:], rh[:].bitcast(F32), cs[0:R, C_NEG:C_NEG + 1],
                                             rx[:], ALU.mult, ALU.add).then_inc(l2w_ready, 1)

                def final(u):
                    b, half = u // NH, u % NH
                    cols = slice(half * HALF, (half + 1) * HALF)
                    bank = bank_of(slot, UNITS + u)
                    dve.wait_ge(l2_ps, UNITS * g + u + 1)
                    if half == 0:
                        if some(16 * g):
                            dve.wait_ge(stored[b], 16 * g)
                    dve.scalar_tensor_tensor(ob[:, b, :, cols], ps[bank][:], 1.0 / DEG,
                                             xs[:, slot, b, :, cols], ALU.mult, ALU.add).then_inc(done, 1)

                at_k = TK * q

                def top_a():
                    dve.wait_ge(fv_copied, GB * (q + 1))
                    dve.memset(fv[:, N:N + PAD], -1.0).then_inc(topk, 1)
                    hold(dve, topk, at_k + 1, 2)
                    dve.max(top[:, 0], fv[:]).then_inc(topk, 1)
                    dve.tensor_scalar(code[:], fv[:, 0:N], 0.0, 2.0, ALU.is_equal, ALU.mult).then_inc(topk, 1)
                    dve.wait_ge(topk, at_k + 3)
                    dve.memset(top[:, 0, 1:8], -1.0).then_inc(topk, 1)
                    dve.tensor_scalar(code[:, U0:U0 + NU], code[:, U0:U0 + NU], 4.0, None, ALU.add
                                      ).then_inc(topk, 1)

                def top_b():
                    hold(dve, topk, at_k + 5, 3)
                    dve.match_replace(fv[:], top[:, 0], fv[:], -2.0).then_inc(topk, 1)
                    hold(dve, topk, at_k + 6, 4)
                    dve.max(top[:, 1], fv[:]).then_inc(topk, 1)

                def top_c():
                    hold(dve, topk, at_k + 7, 5)
                    dve.match_replace(fv[:], top[:, 1], fv[:], -3.0).then_inc(topk, 1)
                    if some(16 * q):
                        dve.wait_ge(t_saved, 16 * q)
                    dve.wait_ge(topk, at_k + 8)
                    dve.tensor_scalar(tr[:], fv[:, 0:N], -3.0, None, ALU.is_equal).then_inc(t_ready, 1)

                def classes():
                    dve.wait_ge(t_ready, q + 1)
                    dve.tensor_tensor(code[:], code[:], tr[:], ALU.add).then_inc(topk, 1)
                    dve.wait_ge(topk, at_k + TK)
                    dve.tensor_scalar(onehot[:, qs], code[:], cs[0:R, C_WANT:C_WANT + 1], None,
                                      ALU.is_equal, ALU.add, accum_out=count[:, qs:qs + 1]
                                      ).then_inc(class_ready, 1)
                    dve.wait_ge(class_ready, q + 1)
                    dve.tensor_scalar(count_r[:, qs], cs[0:R, C_PICK:C_PICK + 2 * GB * NC],
                                      count[:, qs:qs + 1], None, ALU.mult).then_inc(count_ready, 1)

                if prep:
                    stats(0)
                    coefs(0)
                if mid_:
                    top_a()
                    top_b()
                    top_c()
                    classes()
                if prep:
                    stats(1)
                if main:
                    late_sums()
                if prep:
                    coefs(1)
                if mid_:
                    sum_neighbours(0)
                if main:
                    layer2_weights()
                if mid_:
                    sum_neighbours(1)
                if main:
                    final(0)
                    final(1)
                if mid_:
                    middle_a()
                if main:
                    final(2)
                if mid_:
                    middle_b()
                if main:
                    final(3)

            schedule(dve, body)


_OUT = (B, S, N)


def kernel(x, adj, L0_gnn_b1, L0_gnn_b2):
    import numpy as np
    import concourse.bacc as bacc
    from concourse.bass_utils import run_bass_kernel_spmd

    nc = bacc.Bacc("TRN2", target_bir_lowering=False, num_devices=1, dynamic_dma_scratch_size=1024)
    arrays = {
        "x_dram": np.ascontiguousarray(x),
        "adj_t_dram": np.ascontiguousarray(np.asarray(adj).T),
        "b1_dram": np.ascontiguousarray(np.asarray(L0_gnn_b1).reshape(KC, P).T),
        "b2_dram": np.ascontiguousarray(np.asarray(L0_gnn_b2).reshape(1, S)),
        "consts_dram": node_class_constants(),
    }
    args = [nc.dram_tensor(name, a.shape, mybir.dt.from_np(a.dtype), kind="ExternalInput").ap()
            for name, a in arrays.items()]
    out = nc.dram_tensor("out_dram", _OUT, F32, kind="ExternalOutput").ap()
    gnn_kernel(nc, *args, out)
    r = run_bass_kernel_spmd(nc, [arrays], core_ids=[0])
    return r.results[0]["out_dram"]
```

```python
import concourse.bass as bass
from concourse import mybir
from concourse.alu_op_type import AluOpType as ALU
from contextlib import ExitStack

ACT = mybir.ActivationFunctionType
AX = mybir.AxisListType
F32 = mybir.dt.float32
F32R = mybir.dt.float32r
BF16 = mybir.dt.bfloat16

B, S, N = 32, 256, 1024
P = 128
KC = S // P
HALF = 512
NH = N // HALF
GB = 2
NG = B // GB
RING = 3
CH = GB * KC
UNITS = GB * NH
TOPK = 8
NC = 8
ROWS = 32
R = GB * ROWS
PARTS = 2
NU = TOPK
U0 = 1
DEG = float(TOPK + 1)
EPS = 1e-5
BIG = 2.0 ** 100
PAD = 8


def node_class_constants():
    import numpy as np

    lanes = np.arange(R)
    cls, part = lanes % NC, (lanes % ROWS) // NC
    want = np.zeros((P, 2), np.float32)
    want[:R, 0] = cls
    want[:R, 1] = np.where(part == 1, -1, 0)
    const = np.array([DEG, N, DEG, N + 1, DEG, N, 0, N], np.float32)
    coef = np.zeros((NC, NC), np.float32)
    coef[[2, 6], 1] = -1
    coef[[2, 3], 3] = -1
    coef[[2, 6], 4] = 1
    coef[[2, 3, 6, 7, 4, 5], 6] = 1
    pick = np.zeros((P, 2, GB, NC), np.float32)
    for p in range(R):
        if part[p] == 0:
            b = p // ROWS
            pick[p, 0, b, cls[p]] = 1
            pick[p, 1, b, :] = coef[cls[p]]
    base = np.zeros((P, 2, GB, NC), np.float32)
    base[:, 1] = const
    cut = np.zeros((P, P), np.float32)
    cut[:R][(part == 0) & (cls % 4 != 0)] = -BIG
    return np.concatenate([want, pick.reshape(P, -1), base.reshape(P, -1), cut], 1)


FIRST, LAST = -3, NG
LOADS = 4
MID = 10
LATE = 5
TK = 8
NEWTON = 4

C_WANT, C_NEG, C_PICK = 0, 1, 2
C_BASE = C_PICK + 2 * GB * NC
C_CUT = C_BASE + 2 * GB * NC
C_ALL = C_CUT + P


def gnn_kernel(nc, x, adj_t, bias1, bias2, consts, out):
    x_v = x.rearrange("b (k p) n -> b p k n", p=P)
    out_v = out.rearrange("b (k p) n -> b p k n", p=P)
    t_rows = nc.dram_tensor("t_rows", (RING * GB, N), BF16, kind="Internal").ap()

    with ExitStack() as ctx:
        def sb(name, shape, dt=F32):
            return ctx.enter_context(nc.sbuf_tensor(name, shape, dt))

        def sem(name):
            return ctx.enter_context(nc.semaphore(name))

        xs = sb("xs", [P, RING, GB, KC, N])
        hi = sb("hi", [P, RING, GB, KC, N], F32R)
        lo = sb("lo", [P, RING, GB, KC, N], F32R)
        hf = sb("hf", [P, KC, N])
        y1 = sb("y1", [P, 2, KC, HALF])
        ob = sb("ob", [P, GB, KC, N])
        wt = sb("wt", [P, KC, S])
        wh = sb("wh", [P, KC, S], F32R)
        wl = sb("wl", [P, KC, S], F32R)
        cs = sb("cs", [P, C_ALL])
        b1 = sb("b1", [P, KC])
        b2 = sb("b2", [R, S])
        cut = sb("cut", [R, P], F32R)
        sums = sb("sums", [P, P], F32R)
        spare = sb("spare", [P, 8])
        eps = sb("eps", [P, 1])
        ones = sb("ones", [R, P])
        fv = sb("fv", [R, N + PAD])
        top = sb("top", [R, 2, 8])
        code = sb("code", [R, N], BF16)
        tr = sb("tr", [R, N], BF16)
        onehot = sb("onehot", [R, RING, N], F32R)
        count = sb("count", [R, RING])
        count_r = sb("count_r", [R, RING, 2 * GB * NC])
        tmap = sb("tmap", [P, GB, N], BF16)
        junk = sb("junk", [P, KC, N], BF16)
        bn = sb("bn", [P, KC, 2, 6])
        mv = sb("mv", [P, RING, GB, KC, 2])
        std = sb("std", [P, GB, KC])
        nw = sb("nw", [P, 3, KC])
        rstd = sb("rstd", [P, RING, GB, KC])
        nbias = sb("nbias", [P, GB, KC])
        s_all = sb("s_all", [P, RING, GB, KC])
        s_max = sb("s_max", [P, GB, KC])
        s_t = sb("s_t", [P, GB, KC])
        s_u = sb("s_u", [P, 3, GB, KC])
        nd = sb("nd", [P, RING, 2, GB, NC])
        rdeg = sb("rdeg", [P, RING, GB, NC])
        rdeg9 = sb("rdeg9", [P, RING, GB, NC])
        q1 = sb("q1", [P, KC, GB, NC])
        bv = sb("bv", [P, RING, KC, GB, NC])
        v1 = sb("v1", [P, RING, KC, GB, NC])
        nv = sb("nv", [P, KC, GB, NC])
        pt = sb("pt", [P, 6, KC, GB])
        p2 = sb("p2", [P, RING, KC, GB, NC])
        acc = sb("acc", [P, RING, KC, GB, NH + 2])
        yu = sb("yu", [P, GB, KC, NU])
        snk = sb("snk", [P, 3, KC, GB])
        q2 = sb("q2", [P, KC, GB, ROWS])
        rx = sb("rx", [R, S])
        rh = sb("rh", [R, S], F32R)
        l2w = sb("l2w", [R, S], F32R)

        ps = [ctx.enter_context(nc.psum_tensor(f"ps{i}", [P, KC, HALF], F32)) for i in range(3)]
        pf = ctx.enter_context(nc.psum_tensor("pf", [P, N], F32))
        pf_n = pf[:, 0:2 * GB * NC]
        pf_q = pf[:, 64:64 + KC * GB * NC].rearrange("p (m c) -> p m c", m=KC)

        L1_TURN = (1, 3, 4, 5)
        L2_TURN = (6, 7, 2 * UNITS, 2 * UNITS + 2)

        def bank_of(turn, slot, u):
            return (2 * UNITS * slot + turn[u]) % 3

        def q2_bank(slot):
            return ps[bank_of(L1_TURN, slot, UNITS - 1)][0:R, 0, 0:S]

        x_in = [[[sem(f"x_in{s}{b}{k}") for k in range(KC)] for b in range(GB)] for s in range(RING)]
        loaded = sem("loaded")
        const_ready = sem("const_ready")
        b2_ready = sem("b2_ready")
        w_hi = sem("w_hi")
        w_ready = sem("w_ready")
        stats_done = sem("stats_done")
        mv_done = sem("mv_done")
        eps_ready = sem("eps_ready")
        std_ready = sem("std_ready")
        newton = sem("newton")
        coef_ready = sem("coef_ready")
        h_ready = sem("h_ready")
        hi_ready = sem("hi_ready")
        lo_ready = sem("lo_ready")
        fv_ready = sem("fv_ready")
        fv_copied = sem("fv_copied")
        topk = sem("topk")
        t_ready = sem("t_ready")
        class_ready = sem("class_ready")
        count_ready = sem("count_ready")
        t_saved = sem("t_saved")
        t_spread = sem("t_spread")
        st_done = sem("st_done")
        n_ready = sem("n_ready")
        mid = sem("mid")
        q1_ready = sem("q1_ready")
        wq1_ready = sem("wq1_ready")
        bv_ready = sem("bv_ready")
        pool_step = sem("pool_step")
        p2_ready = sem("p2_ready")
        l1_ps = sem("l1_ps")
        l1_out = sem("l1_out")
        yu_scaled = sem("yu_scaled")
        hi2_ready = sem("hi2_ready")
        lo2_ready = sem("lo2_ready")
        late = sem("late")
        q2_ready = sem("q2_ready")
        wq2_ready = sem("wq2_ready")
        l2w_step = sem("l2w_step")
        l2w_ready = sem("l2w_ready")
        l2_ps = sem("l2_ps")
        done = sem("done")
        stored = [sem(f"stored{b}") for b in range(GB)]

        def some(value):
            return not isinstance(value, int) or value > 0

        def is_first(g):
            return isinstance(g, int) and g == 0

        def hold(dve, s, value, column):
            dve.wait_ge(s, value)
            dve.memset(spare[:, column:column + 1], 0.0)

        def group_at(g, slot, lap, d):
            n, s = g + d, slot + d
            if isinstance(n, int) and not 0 <= n < NG:
                return None
            return n, s % RING, lap + s // RING

        def schedule(eng, step):
            def run(g, slot, lap):
                step(lambda d: group_at(g, slot, lap, d))

            laps = (NG - RING) // RING
            for g in range(FIRST, 1):
                run(g, g % RING, g // RING)
            with eng.Fori(0, laps) as i:
                for j in range(1, 1 + RING):
                    run(RING * i + j, j % RING, i + j // RING)
            for g in range(1 + RING * laps, LAST + 1):
                run(g, g % RING, g // RING)

        block = ctx.enter_context(nc.Block())

        @block.sync
        def _(sp):
            def load(g, slot, b):
                for k in range(KC):
                    sp.dma_start(xs[:, slot, b, k], x_v[g * GB + b, :, k]).then_inc(x_in[slot][b][k], 16)

            load(0, 0, 0)
            for dst, src in ((wt[:], adj_t.rearrange("(k p) o -> p k o", p=P)), (cs[:], consts),
                             (b1[:], bias1), (b2[:], bias2.to_broadcast([R, S]))):
                sp.dma_start(dst, src).then_inc(loaded, 16)

            for g in range(RING):
                for b in range(GB):
                    if g + b > 0:
                        load(g, g, b)

            def load_next(group, b):
                g, slot, lap = group
                if not isinstance(g, int) or g + RING < NG:
                    sp.wait_ge(done, UNITS * g + NH * (b + 1))
                    load(g + RING, slot, b)

            def store(group, b):
                g, slot, lap = group
                sp.wait_ge(done, UNITS * g + NH * (b + 1))
                sp.dma_start(out_v[g * GB + b], ob[:, b]).then_inc(stored[b], 16)

            def save_t(group):
                g, slot, lap = group
                sp.wait_ge(t_ready, g + 1)
                sp.dma_start(t_rows[slot * GB:(slot + 1) * GB], tr[0:R:ROWS, :]).then_inc(t_saved, 16)

            def spread_t(group):
                g, slot, lap = group
                sp.wait_ge(t_saved, 16 * (g + 1))
                for b in range(GB):
                    sp.dma_start(tmap[:, b], t_rows[slot * GB + b:slot * GB + b + 1].to_broadcast([P, N])
                                 ).then_inc(t_spread, 16)

            def step(at):
                if at(0):
                    spread_t(at(0))
                if at(-1):
                    load_next(at(-1), 0)
                    store(at(-1), 0)
                    load_next(at(-1), 1)
                    store(at(-1), 1)
                if at(1):
                    save_t(at(1))

            schedule(sp, step)
            for b in range(GB):
                sp.wait_ge(stored[b], 16 * NG)

        @block.tensor
        def _(pe):
            def product(dst, col, rows_hi, rows_lo):
                for k in range(KC):
                    for w, r in ((wh, rows_hi), (wh, rows_lo), (wl, rows_hi)):
                        pe.matmul(dst, w[:, k, col * P:(col + 1) * P], r(k),
                                         start=(k == 0 and w is wh and r is rows_hi), stop=False)

            def unit_main(slot, b, half, bank):
                cols = slice(half * HALF, (half + 1) * HALF)
                for m in range(KC):
                    product(ps[bank][:, m], m, lambda k: hi[:, slot, b, k, cols],
                            lambda k: lo[:, slot, b, k, cols])

            def unit_rows(slot, b, half, bank, rows, signal):
                lanes = slice(b * ROWS, b * ROWS + PARTS * NC)
                for m in range(KC):
                    last = pe.matmul(ps[bank][:, m], rows(lanes, m),
                                     onehot[lanes, slot, half * HALF:(half + 1) * HALF],
                                     start=False, stop=True)
                last.then_inc(signal, 1)

            pe.wait_ge(const_ready, 4)
            pe.wait_ge(w_ready, 1)

            def layer1(group, u):
                g, slot, lap = group
                b, half = u // NH, u % NH
                pe.wait_ge(lo_ready, CH * g + KC * (b + 1))
                if u == 0 and some(g):
                    pe.wait_ge(done, UNITS * g - 3)
                if u == 1 and some(g):
                    pe.wait_ge(done, UNITS * g - 1)
                if u == 2:
                    pe.wait_ge(l1_out, UNITS * g + 1)
                if u == 3 and some(g):
                    pe.wait_ge(done, UNITS * g)
                bank = bank_of(L1_TURN, slot, u)
                unit_main(slot, b, half, bank)
                if u == 0:
                    pe.wait_ge(class_ready, g + 1)
                unit_rows(slot, b, half, bank, lambda lanes, m: cut[lanes, :], l1_ps)

            def layer2(group, u):
                g, slot, lap = group
                pe.wait_ge(lo2_ready, UNITS * g + u + 1)
                if u == 0:
                    pe.wait_ge(l1_out, UNITS * g + 2)
                if u == 1:
                    pe.wait_ge(l1_out, UNITS * g + 3)
                if u == 2:
                    pe.wait_ge(l1_out, UNITS * g + 4)
                    pe.wait_ge(l2w_ready, g + 1)
                if u == 3:
                    pe.wait_ge(done, UNITS * g + 2)
                unit_main(slot, u // NH, u % NH, bank_of(L2_TURN, slot, u))

            def layer2_rows(group, u):
                g, slot, lap = group
                if u == 0:
                    pe.wait_ge(l2w_ready, g + 1)
                unit_rows(slot, u // NH, u % NH, bank_of(L2_TURN, slot, u),
                          lambda lanes, m: l2w[lanes, m * P:(m + 1) * P], l2_ps)

            def class_sizes(group):
                g, slot, lap = group
                if isinstance(g, int) and g in (0, NG - 1):
                    pe.wait_ge(fv_copied, GB * (g + 1))
                else:
                    pe.wait_ge(fv_copied, GB * (g + 1) + 1)
                pe.wait_ge(count_ready, g + 1)
                pe.matmul(pf_n, ones[:, :], count_r[:, slot], start=True, stop=True).then_inc(n_ready, 1)

            def times_q1(group):
                g, slot, lap = group
                pe.wait_ge(q1_ready, 3 * (g + 1))
                for m in range(KC):
                    for k in range(KC):
                        last = pe.matmul(pf_q[:, m], wt[:, k, m * P:(m + 1) * P],
                                         q1[:, k].rearrange("p b c -> p (b c)"),
                                         start=(k == 0), stop=(k == KC - 1))
                last.then_inc(wq1_ready, 1)

            def means(group, b, half):
                g, slot, lap = group
                if some(GB * g + b):
                    pe.wait_ge(fv_copied, GB * g + b)
                if half == 0 and (b == 1 and some(g) or is_first(g - 1)):
                    pe.wait_ge(mid, MID * g)
                pe.wait_ge(lo_ready, CH * g + KC * (b + 1))
                cols = slice(half * HALF, (half + 1) * HALF)
                for k in range(KC):
                    for part, t in enumerate((hi, lo)):
                        last = pe.matmul(pf[:, cols], sums[:], t[:, slot, b, k, cols],
                                         start=(k == 0 and part == 0),
                                         stop=(k == KC - 1 and part == 1))
                last.then_inc(fv_ready, 1)

            def times_q2(group):
                g, slot, lap = group
                pe.wait_ge(q2_ready, KC * (g + 1))
                pe.wait_ge(l1_out, UNITS * (g + 1))
                for k in range(KC):
                    last = pe.matmul(q2_bank(slot), q2[:, k].rearrange("p b c -> p (b c)"), wt[:, k],
                                     start=(k == 0), stop=(k == KC - 1))
                last.then_inc(wq2_ready, 1)

            def step(at):
                if at(1):
                    means(at(1), 1, 1)
                if at(-1):
                    layer2_rows(at(-1), 3)
                if at(1):
                    means(at(1), 1, 0)
                if at(0):
                    if not is_first(at(0)[0]):
                        layer1(at(0), 1)
                    layer1(at(0), 2)
                    layer1(at(0), 3)
                    layer2(at(0), 0)
                    times_q2(at(0))
                    layer2(at(0), 1)
                    layer2_rows(at(0), 0)
                    layer2_rows(at(0), 1)
                    layer2(at(0), 2)
                    layer2_rows(at(0), 2)
                if at(1) and is_first(at(1)[0]):
                    layer1(at(1), 0)
                    class_sizes(at(1))
                    layer1(at(1), 1)
                    means(at(2), 0, 1)
                    times_q1(at(1))
                    means(at(2), 0, 0)
                elif at(2):
                    means(at(2), 0, 1)
                    means(at(2), 0, 0)
                if at(1) and not is_first(at(1)[0]):
                    layer1(at(1), 0)
                    class_sizes(at(1))
                if at(0):
                    layer2(at(0), 3)
                if at(1) and not is_first(at(1)[0]):
                    times_q1(at(1))

            schedule(pe, step)

        @block.scalar
        def _(act):
            act.wait_ge(eps_ready, 1)
            act.activation(spare[:, 6:7], eps[:], ACT.Sqrt)
            act.wait_ge(loaded, 16 * LOADS)
            act.activation(wh[:], wt[:], ACT.Copy).then_inc(w_hi, 1)
            act.activation(cut[:], cs[0:R, C_CUT:C_CUT + P], ACT.Copy).then_inc(const_ready, 1)

            def root(group, b):
                g, slot, lap = group
                act.wait_ge(mv_done, KC * (GB * g + b + 1))
                act.activation(std[:, b], mv[:, slot, b, :, 1], ACT.Sqrt, bias=eps[:]).then_inc(std_ready, 1)

            def h_chunk(group, b, k):
                g, slot, lap = group
                if k == 0:
                    act.wait_ge(coef_ready, GB * g + b + 1)
                if some(CH * g + KC * b + k - 1):
                    act.wait_ge(lo_ready, CH * g + KC * b + k - 1)
                act.activation(hf[:, k], xs[:, slot, b, k], ACT.Relu, bias=nbias[:, b, k:k + 1],
                               scale=rstd[:, slot, b, k:k + 1],
                               accum_out=s_all[:, slot, b, k:k + 1]).then_inc(h_ready, 1)

            def h_hi(group, b, k):
                g, slot, lap = group
                act.wait_ge(h_ready, CH * g + KC * b + k + 1)
                if some(UNITS * (g - RING) + NH * (b + 1)):
                    act.wait_ge(l2_ps, UNITS * (g - RING) + NH * (b + 1))
                act.activation(hi[:, slot, b, k], hf[:, k], ACT.Copy).then_inc(hi_ready, 1)

            def means_copy(group, b):
                g, slot, lap = group
                act.wait_ge(fv_ready, NH * (GB * g + b + 1))
                if b == 0 and some(g):
                    act.wait_ge(t_ready, g)
                lanes = slice(b * ROWS, (b + 1) * ROWS)
                act.activation(fv[lanes, 0:N], pf[lanes, :], ACT.Copy).then_inc(fv_copied, 1)

            def layer1_out(group, u):
                g, slot, lap = group
                b, half = u // NH, u % NH
                bank = bank_of(L1_TURN, slot, u)
                if u == 0:
                    act.wait_ge(bv_ready, g + 1)
                act.wait_ge(l1_ps, UNITS * g + u + 1)
                if some(UNITS * g + u - 1):
                    act.wait_ge(lo2_ready, UNITS * g + u - 1)
                bias = bv[:, slot, :, b]
                first = U0 + NU if half == 0 else 0
                for m in range(KC):
                    last = act.activation(y1[:, u % 2, m, first:], ps[bank][:, m, first:], ACT.Relu,
                                          bias=bias[:, m, 0:1], scale=1.0 / DEG,
                                          accum_out=acc[:, slot, m, b, half:half + 1])
                if half == 0:
                    for m in range(KC):
                        act.activation(y1[:, u % 2, m, 0:U0], ps[bank][:, m, 0:U0], ACT.Relu,
                                       bias=bias[:, m, 0:1], scale=1.0 / DEG,
                                       accum_out=acc[:, slot, m, b, 2:3])
                        last = act.activation(yu[:, b, m], ps[bank][:, m, U0:U0 + NU], ACT.Relu,
                                              bias=bias[:, m, 4:5], scale=rdeg[:, slot, b, 4:5],
                                              accum_out=acc[:, slot, m, b, 3:4])
                last.then_inc(l1_out, 1)

            def y_hi(group, u):
                g, slot, lap = group
                b, half = u // NH, u % NH
                act.wait_ge(l1_out, UNITS * g + u + 1)
                if half == 0:
                    act.activation(y1[:, u % 2, :, U0:U0 + NU], yu[:, b], ACT.Copy,
                                   scale=rdeg9[:, slot, b, 4:5]).then_inc(yu_scaled, 1)
                    act.wait_ge(yu_scaled, GB * g + b + 1)
                act.activation(hi[:, slot, b, :, half * HALF:(half + 1) * HALF], y1[:, u % 2],
                               ACT.Copy).then_inc(hi2_ready, 1)

            def step(at):
                if at(2):
                    h_chunk(at(2), 1, 0)
                    h_hi(at(2), 1, 0)
                    h_chunk(at(2), 1, 1)
                    h_hi(at(2), 1, 1)
                    means_copy(at(2), 0)
                if at(1):
                    layer1_out(at(1), 0)
                if at(2):
                    means_copy(at(2), 1)
                if at(1):
                    y_hi(at(1), 0)
                    layer1_out(at(1), 1)
                    y_hi(at(1), 1)
                if at(3):
                    root(at(3), 0)
                if at(1):
                    layer1_out(at(1), 2)
                    layer1_out(at(1), 3)
                    y_hi(at(1), 2)
                if at(3):
                    h_chunk(at(3), 0, 0)
                    h_hi(at(3), 0, 0)
                    h_chunk(at(3), 0, 1)
                    root(at(3), 1)
                    h_hi(at(3), 0, 1)
                if at(1):
                    y_hi(at(1), 3)

            schedule(act, step)

        @block.gpsimd
        def _(pool):
            pool.memset(eps[:], EPS).then_inc(eps_ready, 1)
            pool.memset(sums[:].bitcast(F32), 1.0).then_inc(const_ready, 1)
            pool.memset(ones[:], 1.0).then_inc(const_ready, 1)
            pool.wait_ge(loaded, 16 * LOADS)
            pool.tensor_scalar(b2[:], b2[:], DEG, None, ALU.mult).then_inc(b2_ready, 1)
            pool.wait_ge(w_hi, 1)
            pool.tensor_tensor(wl[:], wt[:], wh[:].bitcast(F32), ALU.subtract).then_inc(w_ready, 1)

            STEPS = 12

            def h_lo(group, b, k):
                g, slot, lap = group
                pool.wait_ge(hi_ready, CH * g + KC * b + k + 1)
                pool.tensor_tensor(lo[:, slot, b, k], hf[:, k], hi[:, slot, b, k].bitcast(F32),
                                   ALU.subtract).then_inc(lo_ready, 1)

            def y_lo(group, u):
                g, slot, lap = group
                b, cols = u // NH, slice(u % NH * HALF, (u % NH + 1) * HALF)
                pool.wait_ge(hi2_ready, UNITS * g + u + 1)
                pool.tensor_tensor(lo[:, slot, b, :, cols], y1[:, u % 2],
                                   hi[:, slot, b, :, cols].bitcast(F32),
                                   ALU.subtract).then_inc(lo2_ready, 1)

            def class_sums(group):
                g, slot, lap = group
                step = [STEPS * g]

                def add(o, a, b, op=ALU.add):
                    pool.tensor_tensor(o, a, b, op).then_inc(pool_step, 1)
                    step[0] += 1
                    pool.wait_ge(pool_step, step[0])

                n, v, o = nd[:, slot, 0], v1[:, slot], p2[:, slot]
                pool.wait_ge(bv_ready, g + 1)
                for m in range(KC):
                    add(nv[:, m], n, v[:, m], op=ALU.mult)
                add(pt[:, 0], nv[:, :, :, 1], nv[:, :, :, 3])
                add(pt[:, 2], nv[:, :, :, 5], nv[:, :, :, 7])
                add(o[:, :, :, 0], pt[:, 0], pt[:, 2])
                add(o[:, :, :, 1], pt[:, 0], pt[:, 2])
                add(pt[:, 1], nv[:, :, :, 2], nv[:, :, :, 6])
                for c in (4, 5, 7):
                    add(o[:, :, :, c], o[:, :, :, 0], pt[:, 1])
                add(pt[:, 3], pt[:, 2], nv[:, :, :, 6])
                add(o[:, :, :, 2], pt[:, 3], v[:, :, :, 2])
                pool.tensor_tensor(pt[:, 4], nv[:, :, :, 3], pt[:, 1], ALU.add).then_inc(p2_ready, 1)
                pool.tensor_tensor(pt[:, 5], nv[:, :, :, 1], v[:, :, :, 3], ALU.add).then_inc(p2_ready, 1)
                pool.wait_ge(p2_ready, 4 * g + 2)
                pool.tensor_tensor(o[:, :, :, 6], pt[:, 4], pt[:, 2], ALU.add).then_inc(p2_ready, 1)
                pool.tensor_tensor(o[:, :, :, 3], pt[:, 5], pt[:, 3], ALU.add).then_inc(p2_ready, 1)

            def step(at):
                if at(1):
                    h_lo(at(1), 0, 1)
                if at(-1):
                    y_lo(at(-1), 3)
                if at(1):
                    h_lo(at(1), 1, 0)
                    h_lo(at(1), 1, 1)
                if at(0):
                    class_sums(at(0))
                    y_lo(at(0), 0)
                    y_lo(at(0), 1)
                    y_lo(at(0), 2)
                if at(2):
                    h_lo(at(2), 0, 0)

            schedule(pool, step)

        @block.vector
        def _(dve):
            dve.memset(q2[:], 0.0).then_inc(const_ready, 1)

            def stats(group, b, k):
                g, slot, lap = group
                dve.wait_ge(x_in[slot][b][k], 16 * (lap + 1))
                for half in range(2):
                    dve.bn_stats(bn[:, k, half], xs[:, slot, b, k, half * HALF:(half + 1) * HALF]
                                 ).then_inc(stats_done, 1)

            def mean_var(group, b):
                g, slot, lap = group
                hold(dve, stats_done, 4 * (GB * g + b + 1), b)
                for k in range(KC):
                    dve.bn_aggr(mv[:, slot, b, k], bn[:, k].rearrange("p a c -> p (a c)")
                                ).then_inc(mv_done, 1)

            def coefs(group, b):
                g, slot, lap = group
                base = NEWTON * (GB * g + b)
                dve.wait_ge(std_ready, GB * g + b + 1)
                dve.reciprocal(nw[:, 0], std[:, b]).then_inc(newton, 1)
                dve.wait_ge(newton, base + 1)
                dve.scalar_tensor_tensor(nw[:, 1], nw[:, 0], -0.5, nw[:, 0], ALU.mult, ALU.mult
                                         ).then_inc(newton, 1)
                dve.wait_ge(newton, base + 2)
                dve.scalar_tensor_tensor(nw[:, 2], mv[:, slot, b, :, 1], EPS, nw[:, 1],
                                         ALU.add, ALU.mult).then_inc(newton, 1)
                dve.wait_ge(newton, base + 3)
                dve.scalar_tensor_tensor(rstd[:, slot, b], nw[:, 2], 1.5, nw[:, 0],
                                         ALU.add, ALU.mult).then_inc(newton, 1)
                dve.wait_ge(newton, base + NEWTON)
                dve.scalar_tensor_tensor(nbias[:, b], mv[:, slot, b, :, 0], -1.0, rstd[:, slot, b],
                                         ALU.mult, ALU.mult).then_inc(coef_ready, 1)

            def sum_neighbours(group, b, k):
                g, slot, lap = group
                if b == k == 0:
                    dve.wait_ge(t_spread, 16 * GB * (g + 1))
                if some(CH * g + KC * b + k - 1):
                    dve.wait_ge(st_done, CH * g + KC * b + k - 1)
                dve.scalar_tensor_tensor(junk[:, k], xs[:, slot, b, k], mv[:, slot, b, k, 0:1],
                                         tmap[:, b], ALU.max, ALU.mult,
                                         accum_out=s_max[:, b, k:k + 1]).then_inc(st_done, 1)

            def middle_a(group):
                g, slot, lap = group
                base = MID * g
                dve.wait_ge(n_ready, g + 1)
                dve.wait_ge(loaded, 16 * LOADS)
                dve.tensor_tensor(nd[:, slot].rearrange("p a b c -> p (a b c)"), pf_n,
                                  cs[:, C_BASE:C_BASE + 2 * GB * NC], ALU.add).then_inc(mid, 1)
                dve.wait_ge(st_done, CH * (g + 1))
                dve.scalar_tensor_tensor(s_t[:], mv[:, slot, :, :, 0], -float(TOPK), s_max[:],
                                         ALU.mult, ALU.add).then_inc(mid, 1)
                for part, t in enumerate((hi, lo)):
                    dve.tensor_reduce(s_u[:, part], t[:, slot, :, :, U0:U0 + NU].bitcast(F32), AX.X, ALU.add
                                      ).then_inc(mid, 1)
                dve.wait_ge(mid, base + 4)
                dve.reciprocal(rdeg[:, slot], nd[:, slot, 1]).then_inc(mid, 1)
                dve.tensor_tensor(s_t[:], s_t[:], rstd[:, slot], ALU.mult).then_inc(mid, 1)
                dve.tensor_tensor(s_u[:, 2], s_u[:, 0], s_u[:, 1], ALU.add).then_inc(mid, 1)
                dve.wait_ge(mid, base + 7)
                dve.tensor_scalar(rdeg9[:, slot], rdeg[:, slot], DEG, None, ALU.mult).then_inc(mid, 1)
                kb = "p b k -> p k b"
                for src, cols in ((s_t[:], slice(0, NC, 4)), (s_u[:, 2], slice(2, NC, 4)),
                                  (s_all[:, slot], slice(1, NC, 2))):
                    n = NC // (cols.step)
                    dve.tensor_tensor(q1[:, :, :, cols],
                                      src.rearrange(kb).unsqueeze(3).to_broadcast([P, KC, GB, n]),
                                      rdeg[:, slot, :, cols].unsqueeze(1).to_broadcast([P, KC, GB, n]),
                                      ALU.mult).then_inc(q1_ready, 1)

            def middle_b(group):
                g, slot, lap = group
                dve.wait_ge(wq1_ready, g + 1)
                for m in range(KC):
                    dve.tensor_scalar(bv[:, slot, m].rearrange("p b c -> p (b c)"), pf_q[:, m],
                                      b1[:, m:m + 1], None, ALU.add).then_inc(mid, 1)
                dve.wait_ge(mid, MID * (g + 1))
                dve.tensor_scalar(v1[:, slot], bv[:, slot], 0.0, None, ALU.max).then_inc(bv_ready, 1)

            def late_sums(group):
                g, slot, lap = group
                base = LATE * g
                dve.wait_ge(p2_ready, 4 * (g + 1))
                dve.wait_ge(l1_out, UNITS * (g + 1))
                dve.tensor_tensor(snk[:, 0], acc[:, slot, :, :, 0], acc[:, slot, :, :, 1], ALU.add
                                  ).then_inc(late, 1)
                dve.tensor_tensor(snk[:, 1], acc[:, slot, :, :, 2], acc[:, slot, :, :, 3], ALU.add
                                  ).then_inc(late, 1)
                o = p2[:, slot]
                u_sum = acc[:, slot, :, :, 3].unsqueeze(3).to_broadcast([P, KC, GB, 2])
                dve.tensor_tensor(o[:, :, :, 2:NC:4], o[:, :, :, 2:NC:4], u_sum, ALU.add).then_inc(late, 1)
                dve.wait_ge(late, base + 3)
                dve.tensor_tensor(snk[:, 2], snk[:, 0], snk[:, 1], ALU.add).then_inc(late, 1)
                dve.wait_ge(late, base + 4)
                k_sum = snk[:, 2].unsqueeze(3).to_broadcast([P, KC, GB, 4])
                dve.tensor_tensor(o[:, :, :, 1:NC:2], o[:, :, :, 1:NC:2], k_sum, ALU.add).then_inc(late, 1)
                dve.wait_ge(late, base + LATE)
                for k in range(KC):
                    dst = q2[:, k, :, 0:PARTS * NC].rearrange("p b (j c) -> p b j c", j=PARTS)
                    full = [P, GB, PARTS, NC]
                    dve.tensor_tensor(dst, o[:, k].unsqueeze(2).to_broadcast(full),
                                      rdeg9[:, slot].unsqueeze(2).to_broadcast(full), ALU.mult
                                      ).then_inc(q2_ready, 1)

            def layer2_weights(group):
                g, slot, lap = group
                dve.wait_ge(wq2_ready, g + 1)
                dve.wait_ge(b2_ready, 1)
                dve.tensor_tensor(rx[:], q2_bank(slot), b2[:], ALU.add).then_inc(l2w_step, 1)
                dve.wait_ge(l2w_step, 2 * g + 1)
                dve.tensor_copy(rh[:], rx[:]).then_inc(l2w_step, 1)
                dve.wait_ge(l2w_step, 2 * g + 2)
                dve.scalar_tensor_tensor(l2w[:], rh[:].bitcast(F32), cs[0:R, C_NEG:C_NEG + 1],
                                         rx[:], ALU.mult, ALU.add).then_inc(l2w_ready, 1)

            def final(group, u):
                g, slot, lap = group
                b, half = u // NH, u % NH
                cols = slice(half * HALF, (half + 1) * HALF)
                bank = bank_of(L2_TURN, slot, u)
                dve.wait_ge(l2_ps, UNITS * g + u + 1)
                if half == 0 and some(g):
                    dve.wait_ge(stored[b], 16 * g)
                dve.scalar_tensor_tensor(ob[:, b, :, cols], ps[bank][:], 1.0 / DEG,
                                         xs[:, slot, b, :, cols], ALU.mult, ALU.add).then_inc(done, 1)

            def top_a(group):
                g, slot, lap = group
                base = TK * g
                dve.wait_ge(fv_copied, GB * (g + 1))
                dve.memset(fv[:, N:N + PAD], -1.0).then_inc(topk, 1)
                hold(dve, topk, base + 1, 2)
                dve.max(top[:, 0], fv[:]).then_inc(topk, 1)
                dve.tensor_scalar(code[:], fv[:, 0:N], 0.0, -2.0, ALU.is_equal, ALU.mult).then_inc(topk, 1)
                dve.wait_ge(topk, base + 3)
                dve.memset(top[:, 0, 1:8], -1.0).then_inc(topk, 1)
                dve.tensor_scalar(code[:, U0:U0 + NU], code[:, U0:U0 + NU], -4.0, None, ALU.add
                                  ).then_inc(topk, 1)

            def top_b(group):
                g, slot, lap = group
                base = TK * g
                hold(dve, topk, base + 5, 3)
                dve.match_replace(fv[:], top[:, 0], fv[:], -2.0).then_inc(topk, 1)
                hold(dve, topk, base + 6, 4)
                dve.max(top[:, 1], fv[:]).then_inc(topk, 1)

            def top_c(group):
                g, slot, lap = group
                base = TK * g
                hold(dve, topk, base + 7, 5)
                dve.match_replace(fv[:], top[:, 1], fv[:], -3.0).then_inc(topk, 1)
                if some(16 * g):
                    dve.wait_ge(t_saved, 16 * g)
                dve.wait_ge(topk, base + 8)
                dve.tensor_scalar(tr[:], fv[:, 0:N], -3.0, None, ALU.is_equal).then_inc(t_ready, 1)

            def classes(group):
                g, slot, lap = group
                dve.wait_ge(t_ready, g + 1)
                dve.wait_ge(loaded, 16 * LOADS)
                dve.scalar_tensor_tensor(onehot[:, slot], tr[:], cs[0:R, C_WANT:C_WANT + 1], code[:],
                                         ALU.subtract, ALU.is_equal, accum_out=count[:, slot:slot + 1]
                                         ).then_inc(class_ready, 1)
                dve.wait_ge(class_ready, g + 1)
                dve.tensor_scalar(count_r[:, slot], cs[0:R, C_PICK:C_PICK + 2 * GB * NC],
                                  count[:, slot:slot + 1], None, ALU.mult).then_inc(count_ready, 1)

            def step(at):
                if at(-1):
                    final(at(-1), 3)
                if at(2):
                    mean_var(at(2), 0)
                if at(1):
                    top_a(at(1))
                    top_b(at(1))
                if at(2):
                    coefs(at(2), 0)
                if at(1):
                    top_c(at(1))
                if at(2):
                    stats(at(2), 1, 0)
                if at(0):
                    late_sums(at(0))
                if at(2):
                    stats(at(2), 1, 1)
                if at(0):
                    layer2_weights(at(0))
                if at(2):
                    mean_var(at(2), 1)
                if at(1):
                    classes(at(1))
                if at(2):
                    coefs(at(2), 1)
                if at(1):
                    sum_neighbours(at(1), 0, 0)
                if at(0):
                    final(at(0), 0)
                    final(at(0), 1)
                if at(1):
                    sum_neighbours(at(1), 0, 1)
                    sum_neighbours(at(1), 1, 0)
                    sum_neighbours(at(1), 1, 1)
                    middle_a(at(1))
                if at(0):
                    final(at(0), 2)
                if at(1):
                    middle_b(at(1))
                if at(3):
                    stats(at(3), 0, 0)
                    stats(at(3), 0, 1)

            schedule(dve, step)


_OUT = (B, S, N)


def kernel(x, adj, L0_gnn_b1, L0_gnn_b2):
    import numpy as np
    import concourse.bacc as bacc
    from concourse.bass_utils import run_bass_kernel_spmd

    nc = bacc.Bacc("TRN2", target_bir_lowering=False, num_devices=1, dynamic_dma_scratch_size=1024)
    arrays = {
        "x_dram": np.ascontiguousarray(x),
        "adj_t_dram": np.ascontiguousarray(np.asarray(adj).T),
        "b1_dram": np.ascontiguousarray(np.asarray(L0_gnn_b1).reshape(KC, P).T),
        "b2_dram": np.ascontiguousarray(np.asarray(L0_gnn_b2).reshape(1, S)),
        "consts_dram": node_class_constants(),
    }
    args = [nc.dram_tensor(name, a.shape, mybir.dt.from_np(a.dtype), kind="ExternalInput").ap()
            for name, a in arrays.items()]
    out = nc.dram_tensor("out_dram", _OUT, F32, kind="ExternalOutput").ap()
    gnn_kernel(nc, *args, out)
    r = run_bass_kernel_spmd(nc, [arrays], core_ids=[0])
    return r.results[0]["out_dram"]
```
